# Optimizing a Trainium2 kernel written in Bass

```python
import numpy as np
import jax
import jax.numpy as jnp

def _softmax(x, axis=-1):
    return jax.nn.softmax(x, axis=axis)

def _gelu(x):
    return jax.nn.gelu(x, approximate=True)

def _silu(x):
    return jax.nn.silu(x)

def _sigmoid(x):
    return jax.nn.sigmoid(x)

def _layernorm(x, axis=-1, eps=1e-05):
    m = jnp.mean(x, axis=axis, keepdims=True)
    v = jnp.var(x, axis=axis, keepdims=True)
    return (x - m) / jnp.sqrt(v + eps)

def _scatter_add(tgt, idx, src, axis=0):
    return tgt.at[idx].add(src)

def _segment_sum(src, seg, n):
    return jax.ops.segment_sum(src, seg, n)
kernel_name = 'mk_macaron_d1_jaxref_r8_ed549f'

def setup_inputs(seed: int=0):
    np.random.seed(seed)
    _w = jnp.asarray

    def _L0_attn_setup():
        import jax, jax.numpy as jnp
        import numpy as np
        ROPE_THETA = 10000.0
        INF_APPROX = 1e+30
        D_HEAD = 128

        def _rope(x, theta=ROPE_THETA):
            *_, L, D = x.shape
            half = D // 2
            pos = jnp.arange(L, dtype=jnp.float32)[:, None]
            freqs = jnp.power(theta, -jnp.arange(half, dtype=jnp.float32) / half)[None, :]
            angles = pos * freqs
            cos = jnp.cos(angles).astype(x.dtype)
            sin = jnp.sin(angles).astype(x.dtype)
            even, odd = jnp.split(x, 2, axis=-1)
            r_even = even * cos - odd * sin
            r_odd = even * sin + odd * cos
            return jnp.concatenate([r_even, r_odd], axis=-1)
        key = jax.random.key(seed)
        kx, kq, kk, kv, ko = jax.random.split(key, 5)
        B, T, M, D, G, H = (2, 128, 256, 128, 4, 4)
        std_m = M ** (-0.5)
        std_d = D ** (-0.5)
        return {'x': jax.random.normal(kx, (B, T, M), jnp.float32), 'w_aq': jax.random.normal(kq, (G, H, M, D), jnp.float32) * std_m, 'w_ak': jax.random.normal(kk, (G, M, D), jnp.float32) * std_m, 'w_av': jax.random.normal(kv, (G, M, D), jnp.float32) * std_m, 'w_ao': jax.random.normal(ko, (G, H, D, M), jnp.float32) * std_d}
    _L0_attn_in = _L0_attn_setup()

    def _L0_ffn_setup():
        import jax, jax.numpy as jnp
        import numpy as np
        B, S, H = (2, 128, 256)
        I = 128
        E = 32
        Z = 32
        K = 8
        SCALE = 1.5
        CAP = 128
        EPS = 1e-20

        def _moe_forward(x, w_cls, bias, w_gate_up, w_down):
            T = x.shape[0] * x.shape[1]
            xf = x.reshape(T, H)
            logits = xf.astype(jnp.float32) @ w_cls.T
            scores = jax.nn.softmax(logits, axis=-1)
            _, topk_idx = jax.lax.top_k(scores + bias[None, :], K)
            w = jnp.take_along_axis(scores, topk_idx, axis=-1)
            w = w / (w.sum(-1, keepdims=True) + EPS) * SCALE
            routed = topk_idx < E
            w_r = jnp.where(routed, w, 0.0)
            w_z = jnp.where(routed, 0.0, w)
            N = T * K
            flat_ids = jnp.where(routed, topk_idx, E).reshape(-1)
            x_exp = jnp.repeat(xf, K, axis=0)
            order = jnp.argsort(flat_ids)
            ids_s = flat_ids[order]
            counts = jax.ops.segment_sum(jnp.ones(N, jnp.int32), flat_ids, num_segments=E + 1)
            starts = jnp.cumsum(counts) - counts
            pos = jnp.arange(N) - starts[ids_s]
            buf = jnp.zeros((E, CAP, H), xf.dtype).at[ids_s, pos].set(x_exp[order], mode='drop')
            gu = jnp.einsum('ech,ehf->ecf', buf, w_gate_up)
            g, u = jnp.split(gu, 2, axis=-1)
            act = jax.nn.silu(g) * u
            y = jnp.einsum('eci,eih->ech', act, w_down)
            valid = (ids_s < E) & (pos < CAP)
            y_tok = jnp.where(valid[:, None], y[jnp.clip(ids_s, 0, E - 1), jnp.clip(pos, 0, CAP - 1)], 0.0)
            y_exp = jnp.zeros((N, H), xf.dtype).at[order].set(y_tok).reshape(T, K, H)
            routed_out = jnp.einsum('tk,tkh->th', w_r, y_exp)
            out = routed_out * (1.0 + w_z.sum(-1, keepdims=True))
            return out.reshape(x.shape)
        key = jax.random.key(seed)
        ks = jax.random.split(key, 5)
        x = jax.random.normal(ks[0], (B, S, H), jnp.float32)
        w_cls = jax.random.normal(ks[1], (E + Z, H), jnp.float32) / np.float32(np.sqrt(H))
        bias = jax.random.normal(ks[2], (E + Z,), jnp.float32) * 0.02
        w_gate_up = jax.random.normal(ks[3], (E, H, 2 * I), jnp.float32) * 0.02
        w_down = jax.random.normal(ks[4], (E, I, H), jnp.float32) * 0.02
        return {'x': x, 'w_cls': w_cls, 'bias': bias, 'w_gate_up': w_gate_up, 'w_down': w_down}
    _L0_ffn_in = _L0_ffn_setup()
    _d = {'L0_attn_x': _L0_attn_in['x'], 'L0_attn_w_aq': _L0_attn_in['w_aq'], 'L0_attn_w_ak': _L0_attn_in['w_ak'], 'L0_attn_w_av': _L0_attn_in['w_av'], 'L0_attn_w_ao': _L0_attn_in['w_ao'], 'L0_ffn_w_cls': _L0_ffn_in['w_cls'], 'L0_ffn_bias': _L0_ffn_in['bias'], 'L0_ffn_w_gate_up': _L0_ffn_in['w_gate_up'], 'L0_ffn_w_down': _L0_ffn_in['w_down']}
    _x0 = _d['L0_attn_x']
    _d['L0_attn_x'] = jax.random.normal(jax.random.fold_in(jax.random.key(seed), 1), (1, 2048, 256), dtype=_x0.dtype)
    del _x0
    return _d

def reference(L0_attn_x, L0_attn_w_aq, L0_attn_w_ak, L0_attn_w_av, L0_attn_w_ao, L0_ffn_w_cls, L0_ffn_bias, L0_ffn_w_gate_up, L0_ffn_w_down):

    def _L0_attn_ref(x, w_aq, w_ak, w_av, w_ao):
        import jax, jax.numpy as jnp
        import numpy as np
        ROPE_THETA = 10000.0
        INF_APPROX = 1e+30
        D_HEAD = 128

        def _rope(x, theta=ROPE_THETA):
            *_, L, D = x.shape
            half = D // 2
            pos = jnp.arange(L, dtype=jnp.float32)[:, None]
            freqs = jnp.power(theta, -jnp.arange(half, dtype=jnp.float32) / half)[None, :]
            angles = pos * freqs
            cos = jnp.cos(angles).astype(x.dtype)
            sin = jnp.sin(angles).astype(x.dtype)
            even, odd = jnp.split(x, 2, axis=-1)
            r_even = even * cos - odd * sin
            r_odd = even * sin + odd * cos
            return jnp.concatenate([r_even, r_odd], axis=-1)
        B, T, M = x.shape
        q = jnp.einsum('bim,ghmd->bghid', x, w_aq)
        k = jnp.einsum('bim,gmd->bgid', x, w_ak)
        v = jnp.einsum('bim,gmd->bgid', x, w_av)
        q = _rope(q)
        k = _rope(k)
        qk_mult = jnp.asarray(D_HEAD ** (-0.25), dtype=x.dtype)
        s = jnp.einsum('bghid,bgjd->bghij', q * qk_mult, k * qk_mult)
        i = jnp.arange(T)[:, None]
        j = jnp.arange(T)[None, :]
        mask = (i < j).astype(s.dtype)
        s = s - jnp.asarray(INF_APPROX, dtype=s.dtype) * mask
        p = jax.nn.softmax(s, axis=-1)
        o = jnp.einsum('bghij,bgjd->bghid', p, v)
        r = jnp.einsum('bghid,ghdm->bim', o, w_ao)
        return r

    def _L0_ffn_ref(x, w_cls, bias, w_gate_up, w_down):
        import jax, jax.numpy as jnp
        import numpy as np
        B, S, H = (2, 128, 256)
        I = 128
        E = 32
        Z = 32
        K = 8
        SCALE = 1.5
        CAP = 128
        EPS = 1e-20

        def _moe_forward(x, w_cls, bias, w_gate_up, w_down):
            T = x.shape[0] * x.shape[1]
            xf = x.reshape(T, H)
            logits = xf.astype(jnp.float32) @ w_cls.T
            scores = jax.nn.softmax(logits, axis=-1)
            _, topk_idx = jax.lax.top_k(scores + bias[None, :], K)
            w = jnp.take_along_axis(scores, topk_idx, axis=-1)
            w = w / (w.sum(-1, keepdims=True) + EPS) * SCALE
            routed = topk_idx < E
            w_r = jnp.where(routed, w, 0.0)
            w_z = jnp.where(routed, 0.0, w)
            N = T * K
            flat_ids = jnp.where(routed, topk_idx, E).reshape(-1)
            x_exp = jnp.repeat(xf, K, axis=0)
            order = jnp.argsort(flat_ids)
            ids_s = flat_ids[order]
            counts = jax.ops.segment_sum(jnp.ones(N, jnp.int32), flat_ids, num_segments=E + 1)
            starts = jnp.cumsum(counts) - counts
            pos = jnp.arange(N) - starts[ids_s]
            buf = jnp.zeros((E, CAP, H), xf.dtype).at[ids_s, pos].set(x_exp[order], mode='drop')
            gu = jnp.einsum('ech,ehf->ecf', buf, w_gate_up)
            g, u = jnp.split(gu, 2, axis=-1)
            act = jax.nn.silu(g) * u
            y = jnp.einsum('eci,eih->ech', act, w_down)
            valid = (ids_s < E) & (pos < CAP)
            y_tok = jnp.where(valid[:, None], y[jnp.clip(ids_s, 0, E - 1), jnp.clip(pos, 0, CAP - 1)], 0.0)
            y_exp = jnp.zeros((N, H), xf.dtype).at[order].set(y_tok).reshape(T, K, H)
            routed_out = jnp.einsum('tk,tkh->th', w_r, y_exp)
            out = routed_out * (1.0 + w_z.sum(-1, keepdims=True))
            return out.reshape(x.shape)
        return _moe_forward(x, w_cls, bias, w_gate_up, w_down)
    x = L0_attn_x
    x = x + 0.5 * _L0_ffn_ref(_layernorm(x, axis=-1), L0_ffn_w_cls, L0_ffn_bias, L0_ffn_w_gate_up, L0_ffn_w_down)
    x = x + _L0_attn_ref(_layernorm(x, axis=-1), L0_attn_w_aq, L0_attn_w_ak, L0_attn_w_av, L0_attn_w_ao)
    x = x + 0.5 * _L0_ffn_ref(_layernorm(x, axis=-1), L0_ffn_w_cls, L0_ffn_bias, L0_ffn_w_gate_up, L0_ffn_w_down)
    return x

_drawn_inputs = setup_inputs


def setup_inputs(seed=0):
    import zlib

    import numpy as np

    out = dict(_drawn_inputs(seed))
    spreads = {}
    factors = {'L0_ffn_w_cls': 8.0, 'L0_ffn_bias': 8.0, 'L0_ffn_w_gate_up': 8.0, 'L0_ffn_w_down': 8.0}
    for name, (base, spread) in spreads.items():
        noise = np.random.default_rng([zlib.crc32(name.encode()), seed]).standard_normal(out[name].shape)
        drawn = base * np.exp(spread * noise) if base else spread * noise
        out[name] = jnp.asarray(drawn.astype(out[name].dtype))
    for name, factor in factors.items():
        out[name] = (out[name] * factor).astype(out[name].dtype)
    return out
```

```python
from contextlib import ExitStack

import numpy as np

import concourse.bass as bass
from concourse import mybir

F32 = mybir.dt.float32
F32R = mybir.dt.float32r
F16 = mybir.dt.float16
BF16 = mybir.dt.bfloat16
I32 = mybir.dt.int32
U32 = mybir.dt.uint32
ALU = mybir.AluOpType
ACT = mybir.ActivationFunctionType
AX = mybir.AxisListType.X

P = 128
T, M = 2048, 256
NT = T // P
MC = M // P
E, Z, K, CAP = 32, 32, 8, 128
EZ = E + Z
FF = 128
G, H, D = 4, 4, 128
SLOT_SUB = 8
SLOT_HI = CAP // SLOT_SUB
EG = P // SLOT_HI
NG = E // EG
LO_SCALE = 2048.0
RING = 4
EPS_LN, EPS_W, SCALE_W = 1e-5, 1e-20, 1.5
NOT_CHOSEN = 1000.0


class Steps:

    def __init__(self, eng, sem):
        self.eng, self.sem, self.n = eng, sem, 0

    def __call__(self, ins):
        ins.then_inc(self.sem, 1)
        self.n += 1

    def done(self):
        self.eng.wait_ge(self.sem, self.n)


def constants(nc, ctx):
    def sb(name, shape, dt):
        return ctx.enter_context(nc.sbuf_tensor(name, shape, dt))

    c = {}
    c["ident"] = ident = sb("ident", [P, P], F32)
    c["ident16"] = ident16 = sb("ident16", [P, P], BF16)
    c["before"] = before = sb("before", [P, P], BF16)
    c["ones16"] = ones16 = sb("ones16", [P, P], BF16)
    c["future"] = future = sb("future", [P, P], BF16)
    c["iota_hi"] = iota_hi = sb("iota_hi", [P, SLOT_HI], F16)
    c["iota_lo"] = iota_lo = sb("iota_lo", [P, SLOT_SUB], F16)
    c["token"] = token = sb("token", [P, NT, EG], F16)
    c["own"] = own = sb("own", [P, EG], F32)
    made = ctx.enter_context(nc.semaphore("const_made"))
    with nc.Block() as block:

        @block.gpsimd
        def _(pool):
            step = Steps(pool, made)
            step(pool.memset(ident[:, :], 0.0))
            step(pool.memset(ident16[:, :], 0.0))
            step(pool.memset(before[:, :], 1.0))
            step(pool.memset(future[:, :], 0.0))
            step(pool.memset(own[:, :], 1.0))
            step(pool.memset(ones16[:, :], 1.0))
            step(pool.iota(iota_hi[:, :], [[1, SLOT_HI]], base=0, channel_multiplier=0,
                           allow_small_or_imprecise_dtypes=True))
            step(pool.iota(iota_lo[:, :], [[1, SLOT_SUB]], base=0, channel_multiplier=0,
                           allow_small_or_imprecise_dtypes=True))
            step(pool.iota(token[:, :, :], [[P, NT], [0, EG]], base=0, channel_multiplier=1,
                           allow_small_or_imprecise_dtypes=True))
            step.done()
            for t in (ident, ident16):
                step(pool.affine_select(out=t[:, :], in_=t[:, :], compare_op=ALU.not_equal, fill=1.0,
                                        base=0, pattern=[[-1, P]], channel_multiplier=1))
            step(pool.affine_select(out=before[:, :], in_=before[:, :], compare_op=ALU.is_gt, fill=0.0,
                                    base=0, pattern=[[1, P]], channel_multiplier=-1))
            step(pool.affine_select(out=future[:, :], in_=future[:, :], compare_op=ALU.is_ge, fill=-1e30,
                                    base=0, pattern=[[-1, P]], channel_multiplier=1))
            step(pool.affine_select(out=own[:, :], in_=own[:, :], compare_op=ALU.is_ge, fill=0.0,
                                    base=0, pattern=[[-SLOT_HI, EG]], channel_multiplier=1))
            step.done()
            step(pool.affine_select(out=own[:, :], in_=own[:, :], compare_op=ALU.is_ge, fill=0.0,
                                    base=SLOT_HI - 1, pattern=[[SLOT_HI, EG]], channel_multiplier=-1))
            step.done()
    return c


def layernorm(dve, v, x, stats, mv, small, var_ready, root_done, xn, xn_ready):
    for t in range(NT):
        v(dve.bn_stats(stats[:, t, :], x[:, t, :]))
    v.done()
    for t in range(NT):
        v(dve.bn_aggr(mv[:, t, :], stats[:, t, :]))
    v.done()
    var, root, inv, tmp = (small[:, i, :] for i in range(4))
    dve.tensor_scalar(var, mv[:, :, 1], EPS_LN, None, ALU.add).then_inc(var_ready, 1)
    dve.wait_ge(root_done, 1)
    v(dve.reciprocal(inv, root))
    v.done()
    v(dve.tensor_tensor(tmp, inv, inv, ALU.mult))
    v.done()
    v(dve.tensor_tensor(tmp, tmp, var, ALU.mult))
    v.done()
    v(dve.tensor_scalar(tmp, tmp, -0.5, 1.5, ALU.mult, ALU.add))
    v.done()
    v(dve.tensor_tensor(inv, inv, tmp, ALU.mult))
    v.done()
    for t in range(NT):
        ins = dve.tensor_scalar(xn[:, t, :], x[:, t, :], mv[:, t, 0:1], inv[:, t:t + 1],
                                ALU.subtract, ALU.mult)
        if t % (NT // 4) == NT // 4 - 1:
            ins.then_inc(xn_ready, 1)


def ffn(nc, n, c, x, x_dram, w, out):
    top = ExitStack()

    def sb(name, shape, dt, ctx=top):
        return ctx.enter_context(nc.sbuf_tensor(f"{n}_{name}", shape, dt))

    def sem(name):
        return top.enter_context(nc.semaphore(f"{n}_{name}"))

    xn_dram = nc.dram_tensor(f"{n}_xn_dram", (T, M), F32, kind="Internal").ap()
    table_dram = nc.dram_tensor(f"{n}_table_dram", (2, E * CAP), F32, kind="Internal").ap()

    with top:
        psum = [top.enter_context(nc.psum_tensor(f"{n}_bank{i}", [P, 512], F32)) for i in range(2)]
        lg = top.enter_context(nc.psum_tensor(f"{n}_lg", [P, NT, EZ], F32))
        psum += [None, None]
        psum += [top.enter_context(nc.psum_tensor(f"{n}_bank{i}", [P, 512], F32)) for i in range(4, 8)]
        gu_bank = [psum[6], psum[7]]
        y_bank = [psum[4], psum[5]]

        tok = sb("tok", [P, E], F32)
        tok_index = sb("tok_index", [P, E], U32)
        slot_w = sb("slot_w", [P, E], F32)
        wgu = sb("wgu", [P, RING, MC, 2 * FF], F32)
        wd = sb("wd", [P, RING, M], F32)
        rows = sb("rows", [P, RING, M], F32)
        rows_t = sb("rows_t", [P, 2, MC, CAP], F32)
        gate = sb("gate", [P, 2, CAP], F32)
        act_t = sb("act_t", [P, 2, CAP], F32)

        early = ExitStack()
        wcls_raw = sb("wcls_raw", [EZ, M], F32, early)
        wcls_t = sb("wcls_t", [P, MC, EZ], F32, early)
        bias = sb("bias", [P, EZ], F32, early)
        stats = sb("stats", [P, NT, 6], F32, early)
        mv = sb("mv", [P, NT, 2], F32, early)
        small = sb("small", [P, 8, NT], F32, early)
        xn = sb("xn", [P, NT, M], F32, early)
        xn_t = sb("xn_t", [P, MC, T], F32, early)
        score = sb("score", [P, NT, EZ], F32, early)
        biased = sb("biased", [P, NT, EZ], F32, early)
        left = sb("left", [P, NT, EZ], F32, early)
        top8 = sb("top8", [P, NT, K], F32, early)
        mask = sb("mask", [P, NT, EZ], F32, early)
        mask16 = sb("mask16", [P, NT, E], BF16, early)
        unchosen = sb("unchosen", [P, NT, E], F32, early)
        weight = sb("weight", [P, NT, E], F32, early)
        w_hi = sb("w_hi", [P, NT, E], F16, early)
        w_lo = sb("w_lo", [P, NT, E], F16, early)
        pos = sb("pos", [P, NT, E], I32, early)
        part = sb("part", [P, 2, NT, E], I32, early)
        part16 = sb("part16", [P, 2, NT, E], F16, early)
        hot_hi = sb("hot_hi", [P, NT, E, SLOT_HI], F16, early)
        hot_lo = sb("hot_lo", [P, NT, E, SLOT_SUB], F16, early)
        vals = sb("vals", [P, NT, NG, 3, EG * SLOT_SUB], F16, early)
        picked = sb("picked", [P, NG, 3, SLOT_SUB, EG], F32, early)
        summed = sb("summed", [P, NG, 3, SLOT_SUB], F32, early)
        table = sb("table", [P, 2, NG, SLOT_SUB], F32, early)
        table_es = sb("table_es", [2 * E, CAP], F32, early)
        early.close()
        y = sb("y", [P, E, 2, M], F32R)
        hot = sb("hot", [P, 2, E, P], F32R)
        iota_t = sb("iota_t", [P, T], F16)

        x_loaded, w_loaded, step_v, var_ready, root_done = map(sem, ("x_loaded", "w_loaded", "step_v", "var_ready", "root_done"))
        xn_ready, xn_stored, xt_banked, xt_copied = map(sem, ("xn_ready", "xn_stored", "xt_banked", "xt_copied"))
        cls_banked, cls_copied, logits_ready, shifted, exp_done = map(sem, ("cls_banked", "cls_copied", "logits_ready", "shifted", "exp_done"))
        mask_ready, pos_ready, vals_ready, picked_ready, table_ready = map(sem, ("mask_ready", "pos_ready", "vals_ready", "picked_ready", "table_ready"))
        table_stored, table_loaded, slots_banked, slots_ready = map(sem, ("table_stored", "table_loaded", "slots_banked", "slots_ready"))
        gathered = [sem(f"gathered{i}") for i in range(RING)]
        fetched = [sem(f"fetched{i}") for i in range(RING)]
        rt_banked, rt_copied, gu_banked, silu_done, act_ready, y_banked, hi_done, lo_done = map(
            sem, ("rt_banked", "rt_copied", "gu_banked", "silu_done", "act_ready", "y_banked", "hi_done", "lo_done"))
        iota_made, hot_ready, sum_banked, half_added, stored = map(sem, ("iota_made", "hot_ready", "sum_banked", "half_added", "stored"))
        HOT_PARTS = 4
        BODY = RING
        HEAD = 2
        PASSES = (E - HEAD) // BODY

        def expert_steps(eng, first, step):
            first()
            for e in range(HEAD):
                step(e, e)
            with eng.Fori(0, PASSES) as i:
                for k in range(HEAD, HEAD + BODY):
                    step(i * BODY + k, k)
            for e in range(PASSES * BODY + HEAD, E + 1):
                step(e, e % RING)

        block = top.enter_context(nc.Block())

        @block.sync
        def _(sp):
            if x_dram is not None:
                for q in range(4):
                    ts = slice(q * NT // 4, (q + 1) * NT // 4)
                    sp.dma_start(x[:, ts, :], x_dram.rearrange("(t p) m -> p t m", p=P)[:, ts, :]).then_inc(x_loaded, 16)
            sp.dma_start(wcls_raw[:, :], w["cls"]).then_inc(w_loaded, 16)
            sp.dma_start(bias[:, :], w["bias"].rearrange("(a n) -> a n", a=1).to_broadcast([P, EZ])).then_inc(w_loaded, 16)

            def fetch(e, k):
                sp.dma_start(wgu[:, k % RING], w["gate_up"][e].rearrange("(c p) f -> p c f", p=P)).then_inc(fetched[k % RING], 16)
                sp.dma_start(wd[:, k % RING], w["down"][e]).then_inc(fetched[k % RING], 16)

            for e in range(RING):
                fetch(e, e)
            for q in range(4):
                ts = slice(q * NT // 4, (q + 1) * NT // 4)
                sp.wait_ge(xn_ready, q + 1)
                sp.dma_start(xn_dram.rearrange("(t p) m -> p t m", p=P)[:, ts, :], xn[:, ts, :]).then_inc(xn_stored, 16)
            sp.wait_ge(table_ready, 1)
            for v in range(2):
                sp.dma_start(table_dram[v].rearrange("(g p b) -> p g b", g=NG, p=P), table[:, v]).then_inc(table_stored, 16)
            sp.wait_ge(table_stored, 32)
            sp.dma_start(table_es[:, :], table_dram.rearrange("v (e s) -> (v e) s", e=E)).then_inc(table_loaded, 16)
            with sp.Fori(1, E // RING) as i:
                for k in range(RING):
                    sp.wait_ge(y_banked, (i - 1) * RING + k + 1)
                    fetch(i * RING + k, k)
            if out is not None:
                for t in range(0, NT, 2):
                    sp.wait_ge(half_added, 4 + 2 * (t + 2))
                    sp.dma_start(out.rearrange("(t p) m -> p t m", p=P)[:, t:t + 2, :], x[:, t:t + 2, :]).then_inc(stored, 16)
                sp.wait_ge(stored, NT // 2 * 16)

        @block.gpsimd
        def _(pool):
            pool.wait_ge(xn_stored, 64)
            pool.wait_ge(slots_ready, 1)

            for e in range(E):
                if e == 1:
                    pool.iota(iota_t[:, :], [[1, T]], base=0, channel_multiplier=0,
                              allow_small_or_imprecise_dtypes=True).then_inc(iota_made, 1)
                if e >= RING:
                    pool.wait_ge(rt_banked, e - RING + 1)
                pool.indirect_dma_start(
                    out=rows[:, e % RING, :], out_offset=None, in_=xn_dram,
                    in_offset=bass.IndirectOffsetOnAxis(tok_index[:, e:e + 1], 0)).then_inc(gathered[e % RING], 16)

        @block.scalar
        def _(act):
            act.wait_ge(var_ready, 1)
            nc.scalar.activation(small[:, 1, :], small[:, 0, :], ACT.Sqrt).then_inc(root_done, 1)
            act.wait_ge(cls_banked, 1)
            nc.scalar.activation(wcls_t[:, :, :], lg[:, 0:2 * MC // 2, :], ACT.Copy).then_inc(cls_copied, 1)
            for q in range(NT // 2):
                act.wait_ge(xt_banked, q + 1)
                nc.scalar.activation(
                    xn_t[:, :, q * 2 * P:(q + 1) * 2 * P].rearrange("p c (t j) -> p t c j", t=2),
                    psum[q % 2][:, :].rearrange("p (t c j) -> p t c j", t=2, c=MC), ACT.Copy).then_inc(xt_copied, 1)
            act.wait_ge(shifted, 1)
            nc.scalar.activation(score[:, :, :], biased[:, :, :], ACT.Exp).then_inc(exp_done, 1)

            def step(e, k):
                if not (isinstance(e, int) and e == E):
                    act.wait_ge(gu_banked, e + 1)
                    nc.scalar.activation(gate[:, k % 2, :], gu_bank[k % 2][:, 0:CAP], ACT.Silu).then_inc(silu_done, 1)
                if not (isinstance(e, int) and e == 0):
                    act.wait_ge(y_banked, e)
                    nc.scalar.activation(y[:, bass.ds(e - 1, 1), 0, :], y_bank[(k - 1) % 2][:, 0:M], ACT.Copy,
                                         scale=slot_w[:, bass.ds(e - 1, 1)]).then_inc(hi_done, 1)

            act.wait_ge(slots_ready, 1)
            expert_steps(act, lambda: None, step)

        @block.tensor
        def _(pe):
            pe.wait_ge(w_loaded, 32)
            for ch in range(MC):
                ins = pe.transpose(lg[:, ch, :], wcls_raw[:, ch * P:(ch + 1) * P], c["ident"][0:EZ, 0:EZ])
            ins.then_inc(cls_banked, 1)
            for q in range(NT // 2):
                pe.wait_ge(xn_ready, q // 2 + 1)
                if q >= 2:
                    pe.wait_ge(xt_copied, q - 1)
                for t in range(2):
                    for ch in range(MC):
                        ins = pe.transpose(psum[q % 2][:, (t * MC + ch) * P:(t * MC + ch + 1) * P],
                                           xn[:, 2 * q + t, ch * P:(ch + 1) * P], c["ident"][:, :])
                ins.then_inc(xt_banked, 1)
            pe.wait_ge(cls_copied, 1)
            for t in range(NT):
                pe.wait_ge(xt_copied, t // 2 + 1)
                for ch in range(MC):
                    ins = pe.matmul(lg[:, t, :], xn_t[:, ch, t * P:(t + 1) * P], wcls_t[:, ch, :],
                                    start=ch == 0, stop=ch == MC - 1)
            ins.then_inc(logits_ready, 1)
            pe.wait_ge(mask_ready, 1)
            rank = psum[4][:, :].rearrange("p (t e) -> p t e", t=NT)
            pe.matmul(rank, c["before"][:, :], mask16[:, :, :], start=True, stop=False, skip_group_check=True)
            for t in range(NT - 1):
                ins = pe.matmul(rank[:, t + 1:, :], c["ones16"][:, :],
                                mask16[:, t:t + 1, :].to_broadcast([P, NT - 1 - t, E]),
                                start=False, stop=t == NT - 2, skip_group_check=True)
            ins.then_inc(pos_ready, 1)
            pe.wait_ge(vals_ready, 1)
            for g in range(NG):
                for t in range(NT):
                    ins = pe.matmul(psum[5 + g // 2][:, (g % 2) * 256:(g % 2) * 256 + 3 * EG * SLOT_SUB],
                                    hot_hi[:, t, g * EG:(g + 1) * EG, :].rearrange("p e a -> p (e a)"),
                                    vals[:, t, g].rearrange("p v n -> p (v n)"),
                                    start=t == 0, stop=t == NT - 1)
            ins.then_inc(picked_ready, 1)
            pe.wait_ge(table_loaded, 16)
            pe.transpose(psum[4][:, 0:2 * E], table_es[:, :], c["ident"][0:2 * E, 0:2 * E]).then_inc(slots_banked, 1)

            def turn(e, k):
                pe.wait_ge(gathered[k % RING], 16 * (e // RING + 1))
                if isinstance(e, int) and e < 2:
                    pass
                else:
                    pe.wait_ge(rt_copied, e - 1)
                for ch in range(MC):
                    ins = pe.transpose(psum[k % 2][:, ch * P:(ch + 1) * P], rows[:, k % RING, ch * P:(ch + 1) * P],
                                       c["ident"][:, :])
                ins.then_inc(rt_banked, 1)

            def step(e, k):
                last = isinstance(e, int) and e >= E
                if not last:
                    pe.wait_ge(fetched[k % RING], 32 * (e // RING + 1))
                    pe.wait_ge(rt_copied, e + 1)
                    if not (isinstance(e, int) and e < 2):
                        pe.wait_ge(act_ready, e - 1)
                    for half in range(2):
                        for ch in range(MC):
                            ins = pe.matmul(gu_bank[k % 2][:, half * CAP:(half + 1) * CAP],
                                            wgu[:, k % RING, ch, half * FF:(half + 1) * FF], rows_t[:, k % 2, ch, :],
                                            start=ch == 0, stop=ch == MC - 1)
                    ins.then_inc(gu_banked, 1)
                if not (isinstance(e, int) and e >= E - 1):
                    turn(e + 1, k + 1)
                if not (isinstance(e, int) and e == 0):
                    pe.wait_ge(act_ready, e)
                    pe.wait_ge(lo_done, e)
                    pe.matmul(y_bank[(k - 1) % 2][:, 0:M], act_t[:, (k - 1) % 2, :], wd[:, (k - 1) % RING, :],
                              start=True, stop=True).then_inc(y_banked, 1)

            expert_steps(pe, lambda: turn(0, 0), step)

            pe.wait_ge(lo_done, E + 2)
            pe.wait_ge(hi_done, E)
            with pe.Fori(0, NT // 2) as i:
                for k in range(2):
                    t = i * 2 + k
                    pe.wait_ge(half_added, 2 * t + 2)
                    for e in range(E):
                        if e % (E // HOT_PARTS) == 0:
                            pe.wait_ge(hot_ready, t * HOT_PARTS + e // (E // HOT_PARTS) + 1)
                        ins = pe.matmul(psum[k][:, :], hot[:, k, e, :], y[:, e].rearrange("p h m -> p (h m)"),
                                        start=e == 0, stop=e == E - 1)
                    ins.then_inc(sum_banked, 1)

        @block.vector
        def _(dve):
            v = Steps(dve, step_v)
            dve.engine_nop().then_inc(lo_done, 2)
            if x_dram is not None:
                dve.wait_ge(x_loaded, 64)
            layernorm(dve, v, x, stats, mv, small, var_ready, root_done, xn, xn_ready)
            dve.wait_ge(logits_ready, 1)
            big, den, chosen, zero_w = (small[:, i, :] for i in range(4, 8))

            def over(a, width=EZ):
                return a.unsqueeze(2).to_broadcast([P, NT, width])

            v(dve.tensor_reduce(big, lg[:, :, :], AX, ALU.max))
            v.done()
            dve.tensor_tensor(biased[:, :, :], lg[:, :, :], over(big), ALU.subtract).then_inc(shifted, 1)
            dve.wait_ge(exp_done, 1)
            v(dve.tensor_reduce(den, score[:, :, :], AX, ALU.add))
            v.done()
            v(dve.reciprocal(den, den))
            v.done()
            v(dve.tensor_tensor(score[:, :, :], score[:, :, :], over(den), ALU.mult))
            v.done()
            v(dve.tensor_tensor(biased[:, :, :], score[:, :, :],
                                bias[:, :].unsqueeze(1).to_broadcast([P, NT, EZ]), ALU.add))
            v.done()
            for t in range(NT):
                v(dve.max(top8[:, t, :], biased[:, t, :]))
            v.done()
            for t in range(NT):
                v(dve.match_replace(left[:, t, :], top8[:, t, :], biased[:, t, :], -3e38))
            v.done()
            v(dve.tensor_tensor(mask[:, :, :], biased[:, :, :], left[:, :, :], ALU.not_equal))
            v.done()
            dve.tensor_copy(mask16[:, :, :], mask[:, :, 0:E]).then_inc(mask_ready, 1)
            v(dve.tensor_scalar(unchosen[:, :, :], mask[:, :, 0:E], -NOT_CHOSEN, NOT_CHOSEN, ALU.mult, ALU.add))
            v(dve.tensor_tensor(score[:, :, :], score[:, :, :], mask[:, :, :], ALU.mult))
            v.done()
            v(dve.tensor_reduce(chosen, score[:, :, :], AX, ALU.add))
            v(dve.tensor_reduce(zero_w, score[:, :, E:EZ], AX, ALU.add))
            v.done()
            v(dve.tensor_scalar(chosen, chosen, EPS_W, None, ALU.add))
            v.done()
            v(dve.reciprocal(chosen, chosen))
            v.done()
            v(dve.tensor_scalar(chosen, chosen, SCALE_W, None, ALU.mult))
            v.done()
            v(dve.tensor_tensor(zero_w, zero_w, chosen, ALU.mult))
            v.done()
            v(dve.scalar_tensor_tensor(zero_w, zero_w, 1.0, chosen, ALU.add, ALU.mult))
            v.done()
            v(dve.tensor_tensor(weight[:, :, :], score[:, :, 0:E], over(zero_w, E), ALU.mult))
            v.done()
            v(dve.tensor_copy(w_hi[:, :, :], weight[:, :, :]))
            v.done()
            v(dve.tensor_tensor(weight[:, :, :], weight[:, :, :], w_hi[:, :, :], ALU.subtract))
            v.done()
            v(dve.tensor_scalar(w_lo[:, :, :], weight[:, :, :], LO_SCALE, None, ALU.mult))
            dve.wait_ge(pos_ready, 1)
            v(dve.tensor_tensor(pos[:, :, :], psum[4][:, :].rearrange("p (t e) -> p t e", t=NT),
                                unchosen[:, :, :], ALU.add))
            v.done()
            v(dve.tensor_scalar(part[:, 0], pos[:, :, :], SLOT_SUB.bit_length() - 1, None, ALU.arith_shift_right))
            v(dve.tensor_scalar(part[:, 1], pos[:, :, :], SLOT_SUB - 1, None, ALU.bitwise_and))
            v.done()
            v(dve.tensor_copy(part16[:, :, :, :], part[:, :, :, :]))
            v.done()
            v(dve.tensor_tensor(hot_lo[:, :, :, :].rearrange("p t e b -> p (t e) b"),
                                part16[:, 1].rearrange("p t e -> p (t e)").unsqueeze(2).to_broadcast([P, NT * E, SLOT_SUB]),
                                c["iota_lo"][:, :].unsqueeze(1).to_broadcast([P, NT * E, SLOT_SUB]), ALU.is_equal))
            v(dve.tensor_tensor(hot_hi[:, :, :, :].rearrange("p t e a -> p (t e) a"),
                                part16[:, 0].rearrange("p t e -> p (t e)").unsqueeze(2).to_broadcast([P, NT * E, SLOT_HI]),
                                c["iota_hi"][:, :].unsqueeze(1).to_broadcast([P, NT * E, SLOT_HI]), ALU.is_equal))
            v.done()
            lo4 = hot_lo[:, :, :, :].rearrange("p t (g e) b -> p (t g) e b", g=NG)
            for i, val in enumerate((None, w_hi, w_lo)):
                o = vals[:, :, :, i, :].rearrange("p t g (e b) -> p (t g) e b", e=EG)
                if val is None:
                    for g in range(NG):
                        v(dve.tensor_tensor(
                            vals[:, :, g, 0, :].rearrange("p t (e b) -> p t e b", e=EG),
                            hot_lo[:, :, g * EG:(g + 1) * EG, :],
                            c["token"][:, :, :].unsqueeze(3).to_broadcast([P, NT, EG, SLOT_SUB]), ALU.mult))
                else:
                    v(dve.tensor_tensor(
                        o, lo4, val[:, :, :].rearrange("p t (g e) -> p (t g) e", g=NG).unsqueeze(3)
                        .to_broadcast([P, NT * NG, EG, SLOT_SUB]), ALU.mult))
            v.done()
            dve.engine_nop().then_inc(vals_ready, 1)
            dve.wait_ge(picked_ready, 1)
            for g in range(NG):
                v(dve.tensor_tensor(
                    picked[:, g], psum[5 + g // 2][:, (g % 2) * 256:(g % 2) * 256 + 3 * EG * SLOT_SUB]
                    .rearrange("p (v e b) -> p v b e", v=3, e=EG),
                    c["own"][:, :].unsqueeze(1).unsqueeze(1).to_broadcast([P, 3, SLOT_SUB, EG]), ALU.mult))
            v.done()
            v(dve.tensor_reduce(summed[:, :, :, :], picked[:, :, :, :, :].rearrange("p g v b e -> p (g v b) e"), AX, ALU.add))
            v.done()
            v(dve.tensor_copy(table[:, 0], summed[:, :, 0, :]))
            v(dve.scalar_tensor_tensor(table[:, 1], summed[:, :, 2, :], 1.0 / LO_SCALE, summed[:, :, 1, :],
                                       ALU.mult, ALU.add))
            v.done()
            dve.engine_nop().then_inc(table_ready, 1)
            dve.wait_ge(slots_banked, 1)
            v(dve.tensor_copy(tok[:, :], psum[4][:, 0:E]))
            v(dve.tensor_copy(tok_index[:, :], psum[4][:, 0:E]))
            v(dve.tensor_copy(slot_w[:, :], psum[4][:, E:2 * E]))
            v.done()
            dve.engine_nop().then_inc(slots_ready, 1)

            def copy_rows(e, k):
                dve.wait_ge(rt_banked, e + 1)
                if not (isinstance(e, int) and e < 2):
                    dve.wait_ge(gu_banked, e - 1)
                dve.tensor_copy(rows_t[:, k % 2], psum[k % 2][:, 0:M].rearrange("p (c s) -> p c s", c=MC)).then_inc(rt_copied, 1)

            def step(e, k):
                if not (isinstance(e, int) and e >= E):
                    dve.wait_ge(silu_done, e + 1)
                    if not (isinstance(e, int) and e < 2):
                        dve.wait_ge(y_banked, e - 1)
                    dve.tensor_tensor(act_t[:, k % 2, :], gate[:, k % 2, :], gu_bank[k % 2][:, CAP:2 * CAP],
                                      ALU.mult).then_inc(act_ready, 1)
                if not (isinstance(e, int) and e >= E - 1):
                    copy_rows(e + 1, k + 1)
                if not (isinstance(e, int) and e == 0):
                    dve.wait_ge(hi_done, e)
                    dve.scalar_tensor_tensor(y[:, bass.ds(e - 1, 1), 1, :], y_bank[(k - 1) % 2][:, 0:M],
                                             slot_w[:, bass.ds(e - 1, 1)], y[:, bass.ds(e - 1, 1), 0, :].bitcast(F32),
                                             ALU.mult, ALU.subtract).then_inc(lo_done, 1)

            expert_steps(dve, lambda: copy_rows(0, 0), step)

            dve.wait_ge(iota_made, 1)
            dve.wait_ge(lo_done, E + 2)
            dve.engine_nop().then_inc(half_added, 4)
            PART = E // HOT_PARTS

            def make_hot(t, k):
                for e in range(E):
                    ins = dve.tensor_scalar(hot[:, k, e, :], iota_t[:, bass.ds(t * P, P)], tok[:, e:e + 1], None, ALU.is_equal)
                    if e % PART == PART - 1:
                        ins.then_inc(hot_ready, 1)

            def add_sum(t, k):
                dve.wait_ge(sum_banked, t + 1)
                for half in (1, 0):
                    ins = dve.scalar_tensor_tensor(x[:, bass.ds(t, 1), :], psum[k][:, half * M:(half + 1) * M], 0.5,
                                                   x[:, bass.ds(t, 1), :], ALU.mult, ALU.add)
                    ins.then_inc(half_added, 1)
                    dve.wait_ge(half_added, 4 + 2 * t + (1 if half else 2))

            make_hot(0, 0)
            make_hot(1, 1)
            with dve.Fori(0, NT // 2 - 1) as i:
                for k in range(2):
                    add_sum(i * 2 + k, k)
                    make_hot(i * 2 + k + 2, k)
            add_sum(NT - 2, 0)
            add_sum(NT - 1, 1)


NB = 4
BW = NB * P
BLOCKS = T // BW
CHUNKS = NB * BLOCKS * (BLOCKS + 1) // 2
ITEMS = CHUNKS
ADDS = 2 * BLOCKS
SLOTS = 3
LAG = 2
ROWS = NB * BLOCKS
STATS = 8


def chunk_no(a, ch):
    return sum(r // NB + 1 for r in range(a)) + ch


def item_no(i, j):
    return NB * i * (i + 1) // 2 + j


def head_plan():
    plan = []
    waiting = {"E": [], "N": [], "V": []}

    def flush_exp(n):
        for _ in range(min(n, len(waiting["E"]))):
            plan.append(waiting["E"].pop(0))

    def scores(a, nxt=0):
        flush_exp(99)
        plan.append(("S", (a,), nxt))
        while waiting["N"]:
            plan.append(waiting["N"].pop(0))
        waiting["E"] += [("E", (a, ch), nxt) for ch in range(a // NB + 1)]
        flush_exp(2)
        waiting["N"].append(("N", (a,), nxt))

    def value(n):
        for _ in range(n):
            v = waiting["V"].pop(0)
            plan.append(v)
            i, j = v[1]
            if j == NB * (i + 1) - 1:
                plan.append(("O", (i,), 0))

    def items(i, js):
        for j in js:
            plan.append(("T", (i, j), 0))
            waiting["V"].append(("V", (i, j), 0))
            if len(waiting["V"]) > LAG:
                value(1)
            if waiting["E"]:
                flush_exp(1)
            elif waiting["N"]:
                plan.append(waiting["N"].pop(0))

    def output(i):
        plan.extend([("R", (i, 0), 0), ("R", (i, 1), 0)])

    def cuts(n, parts):
        return [list(range(n * p // parts, n * (p + 1) // parts)) for p in range(parts)]

    plan.append(("WO", (), 0))
    for i in range(BLOCKS - 1):
        n = NB * (i + 1)
        groups = cuts(n, NB) if i else [[0, 1], [2, 3], [], []]
        if i > 1:
            groups = [[0, 1]] + [[j + 2 for j in g] for g in cuts(n - 2, NB - 1)]
        for q in range(NB):
            scores(NB * (i + 1) + q)
            items(i, groups[q])
            if q == 1 and i:
                output(i - 1)
            if q == 2 and i == 1:
                plan.append(("WQ", (), 1))
    body = list(plan)
    plan.clear()
    i, n = BLOCKS - 1, NB * BLOCKS
    saved = {k: list(v) for k, v in waiting.items()}

    def tail(kind):
        plan.clear()
        for k in waiting:
            waiting[k] = list(saved[k])
        flush_exp(99)
        if kind == "last":
            while waiting["N"]:
                plan.append(waiting["N"].pop(0))
            items(i, range(0, 6))
            output(i - 1)
            items(i, range(6, n))
            value(len(waiting["V"]))
            output(i)
            return list(plan)
        xs = [("Q", ch) for ch in range(BLOCKS)]
        if kind == "edge":
            xs = [("K", ch) for ch in range(BLOCKS)] + xs
        before = None
        at = 0
        for m, x in enumerate(xs):
            if x == ("K", 0):
                plan.append(("WKV", ("K",), 1))
            plan.append(("X", x, 1))
            while waiting["N"]:
                plan.append(waiting["N"].pop(0))
            items(i, range(at, at + 2))
            at += 2
            if m == 1:
                output(i - 1)
            if before:
                plan.append(("Y", before, 1))
            before = x
        plan.append(("Y", before, 1))
        if kind == "edge":
            value(len(waiting["V"]))
            plan.append(("WKV", ("V",), 1))
            for ch in range(BLOCKS):
                plan.append(("XV", (ch,), 1))
            for q in range(NB):
                scores(q, 1)
            flush_exp(99)
        else:
            groups = [range(8, 10), range(10, 13), range(13, 16), []]
            for q in range(NB):
                scores(q, 1)
                items(i, groups[q])
                if q == 2:
                    value(len(waiting["V"]))
            flush_exp(99)
        while waiting["N"]:
            plan.append(waiting["N"].pop(0))
        output(i)
        return list(plan)

    return body, {kind: tail(kind) for kind in ("next", "edge", "last")}


def opening_plan():
    plan = [("WKV", ("K",), 0)]
    order = [("K", ch) for ch in range(BLOCKS)]
    for m, x in enumerate(order):
        plan.append(("X", x, 0))
        if m:
            plan.append(("Y", order[m - 1], 0))
    plan += [("Y", order[-1], 0), ("WQ", (), 0)]
    order = [("Q", ch) for ch in range(BLOCKS)]
    for m, x in enumerate(order):
        plan.append(("X", x, 0))
        if m:
            plan.append(("Y", order[m - 1], 0))
    plan += [("Y", order[-1], 0), ("WKV", ("V",), 0)]
    plan += [("XV", (ch,), 0) for ch in range(BLOCKS)]
    for q in range(NB):
        plan += [("S", (q,), 0), ("E", (q, 0), 0)]
        plan += [("N", (q,), 0)]
    return plan


def bank_uses(plan):
    return [s[:2] for s in plan if s[0] in ("T", "R")]


def attention(nc, c, x, w, cos_dram, sin_dram):
    top = ExitStack()

    def sb(name, shape, dt, ctx=top):
        return ctx.enter_context(nc.sbuf_tensor(f"at_{name}", shape, dt))

    def sem(name):
        return top.enter_context(nc.semaphore(f"at_{name}"))

    body, tails = head_plan()
    uses = {kind: bank_uses(body + tail) for kind, tail in tails.items()}
    last = [("T", (BLOCKS - 1, ROWS - 1)), ("R", (BLOCKS - 1, 0)), ("R", (BLOCKS - 1, 1))]
    assert all(len(u) % SLOTS == 0 and u[-SLOTS:] == last for u in uses.values())

    with top:
        s_bank = [top.enter_context(nc.psum_tensor(f"at_s{i}", [P, BW], F32)) for i in range(BLOCKS)]
        t_bank = [top.enter_context(nc.psum_tensor(f"at_t{i}", [P, BW], F32)) for i in range(SLOTS)]
        o_bank = top.enter_context(nc.psum_tensor("at_o", [P, BW], F32))

        xt = sb("xt", [P, 2, MC, T], F32R)
        kt = sb("kt", [P, 2, T], F32R)
        qt = sb("qt", [P, 2, T], F32R)
        vv = sb("vv", [P, 2, NT, D], F32R)
        cos = sb("cos", [P, T], F32)
        sin = sb("sin", [P, T], F32)
        pt = sb("pt", [P, SLOTS, 2, BW], F32R)
        ot = sb("ot", [P, 2, BW], F32R)
        swapped = sb("swapped", [P, 2, BW], F32)
        turned = sb("turned", [P, 2, BW], F32)
        wq_raw = sb("wq_raw", [P, MC, D], F32)
        wq = sb("wq", [P, 2, MC, D], F32R)
        wkv_raw = sb("wkv_raw", [P, MC, D], F32)
        wkv = sb("wkv", [P, 2, MC, D], F32R)
        wo_raw = sb("wo_raw", [P, M], F32)
        wo = sb("wo", [P, 2, M], F32R)
        row_max = sb("row_max", [P, STATS, BLOCKS], F32)
        neg_max = sb("neg_max", [P, STATS], F32)
        row_sum = sb("row_sum", [P, STATS, BLOCKS], F32)
        inv_sum = sb("inv_sum", [P, STATS], F32)
        early = ExitStack()
        xn = sb("xn", [P, NT, M], F32, early)
        stats = sb("stats", [P, NT, 6], F32, early)
        mv = sb("mv", [P, NT, 2], F32, early)
        small = sb("small", [P, 4, NT], F32, early)
        early.close()
        prob = [sb("prob0", [P, NB, (BLOCKS - 1) * BW], F32), sb("prob1", [P, NB, BLOCKS * BW], F32)]

        step_v, var_ready, root_done, xn_ready, xt_banked, xt_hi, xt_lo = map(
            sem, ("step_v", "var_ready", "root_done", "xn_ready", "xt_banked", "xt_hi", "xt_lo"))
        tables_loaded, wq_loaded, wkv_loaded, wo_loaded = map(sem, ("tables_loaded", "wq_loaded", "wkv_loaded", "wo_loaded"))
        wq_split, wkv_split, wo_split, split_hi = map(sem, ("wq_split", "wkv_split", "wo_split", "split_hi"))
        x_banked, x_swapped, x_cos, x_sin, x_turned, x_hi, x_lo = map(
            sem, ("x_banked", "x_swapped", "x_cos", "x_sin", "x_turned", "x_hi", "x_lo"))
        v_banked, v_hi, v_lo = map(sem, ("v_banked", "v_hi", "v_lo"))
        s_banked, max_part, max_ready, exp_done, sum_part, inv_ready, normed = map(
            sem, ("s_banked", "max_part", "max_ready", "exp_done", "sum_part", "inv_ready", "normed"))
        t_banked, t_hi, t_lo, pv_done, o_hi, o_lo, r_banked = map(
            sem, ("t_banked", "t_hi", "t_lo", "pv_done", "o_hi", "o_lo", "r_banked"))
        r_added = sem("r_added")

        XG = BLOCKS * (1 + H)

        def walk(eng, steps):
            steps(opening_plan(), "next", 0, 0, 0)
            with eng.Fori(0, G - 1) as g:
                with eng.Fori(0, H - 1) as h:
                    steps(body + tails["next"], "next", g * H + h, g, h)
                steps(body + tails["edge"], "edge", g * H + H - 1, g, H - 1)
            with eng.Fori(0, H - 1) as h:
                steps(body + tails["next"], "next", (G - 1) * H + h, G - 1, h)
            steps(body + tails["last"], "last", G * H - 1, G - 1, H - 1)

        def bank_of(kind, step):
            return uses[kind].index(step) % SLOTS

        def wait_bank(eng, kind, step, hh):
            n = uses[kind].index(step) - SLOTS
            before, back = (uses[kind][n], 0) if n >= 0 else (last[n], 1)
            if before[0] == "T":
                eng.wait_ge(t_lo, (hh - back) * ITEMS + item_no(*before[1]) + 2)
            else:
                eng.wait_ge(r_added, (hh - back) * ADDS + 2 * before[1][0] + before[1][1] + 3)

        def chunk_at(kind, what, ch, g, h, nxt):
            if kind == "edge" and nxt:
                g, h = g + 1, 0
            elif nxt:
                h = h + 1
            return g * XG + ch if what == "K" else g * XG + BLOCKS + h * BLOCKS + ch

        block = top.enter_context(nc.Block())

        @block.sync
        def _(sp):
            sp.dma_start(cos[:, :], cos_dram).then_inc(tables_loaded, 16)
            sp.dma_start(sin[:, :], sin_dram).then_inc(tables_loaded, 16)

            def load_kv(which, g):
                sp.dma_start(wkv_raw[:, :, :], w[which][g].rearrange("(c p) d -> p c d", p=P)).then_inc(wkv_loaded, 16)

            def load_q(hh):
                sp.dma_start(wq_raw[:, :, :], w["q"].rearrange("g h (c p) d -> (g h) p c d", p=P)[hh]).then_inc(wq_loaded, 16)

            def load_o(hh):
                sp.dma_start(wo_raw[:, :], w["o"].rearrange("g h d m -> (g h) d m")[hh]).then_inc(wo_loaded, 16)

            load_kv("k", 0)
            load_q(0)
            load_o(0)
            sp.wait_ge(wkv_split, 1)
            load_kv("v", 0)

            def load_next(hh):
                sp.wait_ge(wq_split, hh + 1)
                load_q(hh + 1)
                sp.wait_ge(wo_split, hh + 1)
                load_o(hh + 1)

            with sp.Fori(0, G - 1) as g:
                with sp.Fori(0, H) as h:
                    load_next(g * H + h)
                sp.wait_ge(wkv_split, 2 * g + 2)
                load_kv("k", g + 1)
                sp.wait_ge(wkv_split, 2 * g + 3)
                load_kv("v", g + 1)
            with sp.Fori(0, H - 1) as h:
                load_next((G - 1) * H + h)

        @block.gpsimd
        def _(pool):
            pool.wait_ge(tables_loaded, 32)

            def steps(plan, kind, hh, g, h):
                for what, which, nxt in plan:
                    if what == "X":
                        n = chunk_at(kind, which[0], which[1], g, h, nxt)
                        r = which[1] % 2
                        cs = slice(which[1] * BW, (which[1] + 1) * BW)
                        pool.wait_ge(x_swapped, 2 * (n + 1))
                        pool.tensor_tensor(swapped[:, r, :], swapped[:, r, :], sin[:, cs], ALU.mult).then_inc(x_sin, 1)
                        pool.wait_ge(x_sin, n + 1)
                        pool.wait_ge(x_cos, n + 1)
                        pool.tensor_tensor(turned[:, r, :], turned[:, r, :], swapped[:, r, :], ALU.add).then_inc(x_turned, 1)
                    elif what == "N":
                        a, = which
                        pr = prob[(a // NB) % 2][:, a % NB, 0:(a + 1) * P]
                        pool.wait_ge(inv_ready, (hh + nxt) * ROWS + a + 1)
                        pool.tensor_tensor(pr, pr, inv_sum[:, a % STATS:a % STATS + 1].to_broadcast([P, (a + 1) * P]),
                                           ALU.mult).then_inc(normed, 1)

            walk(pool, steps)

        @block.scalar
        def _(act):
            act.wait_ge(var_ready, 1)
            nc.scalar.activation(small[:, 1, :], small[:, 0, :], ACT.Sqrt).then_inc(root_done, 1)
            for q in range(NT // 2):
                act.wait_ge(xt_banked, q + 1)
                nc.scalar.activation(xt[:, 0, :, q * 2 * P:(q + 1) * 2 * P].rearrange("p c (t j) -> p t c j", t=2),
                                     s_bank[q % BLOCKS][:, :].rearrange("p (t c j) -> p t c j", t=2, c=MC),
                                     ACT.Copy).then_inc(xt_hi, 1)

            def steps(plan, kind, hh, g, h):
                for what, which, nxt in plan:
                    if what == "X":
                        n = chunk_at(kind, which[0], which[1], g, h, nxt)
                        r = which[1] % 2
                        act.wait_ge(x_banked, n + 1)
                        act.wait_ge(x_hi, n + 1)
                        for half in range(2):
                            nc.scalar.activation(swapped[half * 64:half * 64 + 64, r, :],
                                                 s_bank[which[1]][64 - half * 64:128 - half * 64, :],
                                                 ACT.Copy).then_inc(x_swapped, 1)
                    elif what == "Y":
                        n = chunk_at(kind, which[0], which[1], g, h, nxt)
                        dst = kt if which[0] == "K" else qt
                        act.wait_ge(x_turned, n + 1)
                        nc.scalar.activation(dst[:, 0, which[1] * BW:(which[1] + 1) * BW], turned[:, which[1] % 2, :],
                                             ACT.Copy).then_inc(x_hi, 1)
                    elif what == "XV":
                        ch, = which
                        gg = g + nxt
                        act.wait_ge(v_banked, gg * BLOCKS + ch + 1)
                        nc.scalar.activation(vv[:, 0, ch * NB:(ch + 1) * NB, :],
                                             s_bank[ch][:, :].rearrange("p (t d) -> p t d", t=NB), ACT.Copy).then_inc(v_hi, 1)
                    elif what == "E":
                        a, ch = which
                        width = min(BW, (a + 1) * P - ch * BW)
                        act.wait_ge(max_ready, (hh + nxt) * ROWS + a + 1)
                        nc.scalar.activation(prob[(a // NB) % 2][:, a % NB, ch * BW:ch * BW + width],
                                             s_bank[ch][:, 0:width], ACT.Exp, bias=neg_max[:, a % STATS:a % STATS + 1],
                                             accum_out=row_sum[:, a % STATS, ch:ch + 1]).then_inc(exp_done, 1)
                    elif what == "T":
                        i, j = which
                        c0 = max(j - NB * i, 0) * P
                        act.wait_ge(t_banked, hh * ITEMS + item_no(i, j) + 1)
                        nc.scalar.activation(pt[:, item_no(i, j) % SLOTS, 0, c0:], t_bank[bank_of(kind, (what, which))][:, c0:],
                                             ACT.Copy).then_inc(t_hi, 1)
                    elif what == "O":
                        act.wait_ge(pv_done, hh * ITEMS + item_no(which[0], NB * (which[0] + 1) - 1) + 1)
                        nc.scalar.activation(ot[:, 0, :], o_bank[:, :], ACT.Copy).then_inc(o_hi, 1)

            walk(act, steps)

        @block.tensor
        def _(pe):
            for q in range(NT // 2):
                pe.wait_ge(xn_ready, q // 2 + 1)
                if q >= BLOCKS:
                    pe.wait_ge(xt_lo, q - BLOCKS + 1)
                for t in range(2):
                    for ch in range(MC):
                        ins = pe.transpose(s_bank[q % BLOCKS][:, (t * MC + ch) * P:(t * MC + ch + 1) * P],
                                           xn[:, 2 * q + t, ch * P:(ch + 1) * P], c["ident"][:, :])
                ins.then_inc(xt_banked, 1)
            pe.wait_ge(xt_lo, NT // 2)

            PAIRS = ((0, 0), (0, 1), (1, 0))

            def steps(plan, kind, hh, g, h):
                for what, which, nxt in plan:
                    if what == "X":
                        which_w, ch = which
                        n = chunk_at(kind, which_w, ch, g, h, nxt)
                        if ch == 0:
                            if which_w == "K":
                                pe.wait_ge(wkv_split, 2 * (g + nxt) + 1)
                            else:
                                pe.wait_ge(wq_split, hh + nxt + 1)
                        if nxt:
                            pe.wait_ge(exp_done, (hh + 1) * CHUNKS)
                        if which_w == "Q":
                            if kind == "edge" or not nxt:
                                pe.wait_ge(x_cos, n - BLOCKS + 1)
                        ws = wkv if which_w == "K" else wq
                        for m, (wi, xi) in enumerate(PAIRS):
                            for mc in range(MC):
                                ins = pe.matmul(s_bank[ch][:, :], ws[:, wi, mc, :], xt[:, xi, mc, ch * BW:(ch + 1) * BW],
                                                start=m == 0 and mc == 0, stop=m == 2 and mc == MC - 1)
                        ins.then_inc(x_banked, 1)
                    elif what == "XV":
                        ch, = which
                        gg = g + nxt
                        if ch == 0:
                            pe.wait_ge(wkv_split, 2 * gg + 2)
                        pe.wait_ge(x_cos, (gg * XG + BLOCKS) + ch + 1)
                        for t in range(NB):
                            for m, (xi, wi) in enumerate(PAIRS):
                                for mc in range(MC):
                                    tt = ch * NB + t
                                    ins = pe.matmul(s_bank[ch][:, t * D:(t + 1) * D], xt[:, xi, mc, tt * P:(tt + 1) * P],
                                                    wkv[:, wi, mc, :], start=m == 0 and mc == 0, stop=m == 2 and mc == MC - 1)
                        ins.then_inc(v_banked, 1)
                    elif what == "S":
                        a, = which
                        i = a // NB
                        if a % NB == 0:
                            n = (g * XG + BLOCKS + h * BLOCKS + i) if not nxt else chunk_at(kind, "Q", i, g, h, 1)
                            pe.wait_ge(x_lo, n + 3)
                            if i == 0:
                                pe.wait_ge(v_lo, (g + (1 if nxt and kind == "edge" else 0) + 1) * BLOCKS)
                        for ch in range(i + 1):
                            width = min(BW, (a + 1) * P - ch * BW)
                            if a % NB or ch < i:
                                pe.wait_ge(exp_done, (hh + nxt) * CHUNKS + chunk_no(a - 1, ch) + 1)
                            out = s_bank[ch][:, 0:width]
                            for m, (qi, ki) in enumerate(PAIRS):
                                ins = pe.matmul(out, qt[:, qi, a * P:(a + 1) * P], kt[:, ki, ch * BW:ch * BW + width],
                                                start=m == 0, stop=m == 2 and ch < i)
                            if ch == i:
                                ins = pe.matmul(s_bank[ch][:, width - P:width], c["ident16"][:, :], c["future"][:, :],
                                                start=False, stop=True)
                            ins.then_inc(s_banked, 1)
                    elif what == "T":
                        i, j = which
                        bank = t_bank[bank_of(kind, (what, which))]
                        if j == 0:
                            pe.wait_ge(normed, hh * ROWS + (i + 1) * NB)
                        wait_bank(pe, kind, (what, which), hh)
                        for r in range(max(j - NB * i, 0), NB):
                            ins = pe.transpose(bank[:, r * P:(r + 1) * P],
                                               prob[i % 2][:, r, j * P:(j + 1) * P], c["ident"][:, :])
                        ins.then_inc(t_banked, 1)
                    elif what == "V":
                        i, j = which
                        slot = item_no(i, j) % SLOTS
                        c0 = max(j - NB * i, 0) * P
                        if j == 0:
                            pe.wait_ge(o_lo, hh * BLOCKS + i + 1)
                        pe.wait_ge(t_lo, hh * ITEMS + item_no(i, j) + 2)
                        for m, (vi, pi) in enumerate(PAIRS):
                            ins = pe.matmul(o_bank[:, c0:], vv[:, vi, j, :], pt[:, slot, pi, c0:],
                                            start=m == 0 and j == 0, stop=m == 2 and j == NB * (i + 1) - 1)
                        ins.then_inc(pv_done, 1)
                    elif what == "R":
                        i, half = which
                        bank = t_bank[bank_of(kind, (what, which))]
                        if half == 0:
                            pe.wait_ge(o_lo, hh * BLOCKS + i + 2)
                            if i == 0:
                                pe.wait_ge(wo_split, hh + 1)
                        wait_bank(pe, kind, (what, which), hh)
                        for t in range(2):
                            tt = half * 2 + t
                            for m, (oi, wi) in enumerate(PAIRS):
                                ins = pe.matmul(bank[:, t * M:(t + 1) * M], ot[:, oi, tt * P:(tt + 1) * P],
                                                wo[:, wi, :], start=m == 0, stop=m == 2)
                        ins.then_inc(r_banked, 1)

            walk(pe, steps)

        @block.vector
        def _(dve):
            v = Steps(dve, step_v)
            dve.engine_nop().then_inc(o_lo, 1)
            dve.engine_nop().then_inc(r_banked, 1)
            dve.engine_nop().then_inc(t_lo, 1)
            dve.engine_nop().then_inc(r_added, 2)
            dve.engine_nop().then_inc(x_hi, 2)
            dve.engine_nop().then_inc(x_lo, 2)
            layernorm(dve, v, x, stats, mv, small, var_ready, root_done, xn, xn_ready)
            for q in range(NT // 2):
                dve.wait_ge(xt_hi, q + 1)
                cols = slice(q * 2 * P, (q + 1) * 2 * P)
                dve.tensor_tensor(xt[:, 1, :, cols].rearrange("p c (t j) -> p t c j", t=2),
                                  s_bank[q % BLOCKS][:, :].rearrange("p (t c j) -> p t c j", t=2, c=MC),
                                  xt[:, 0, :, cols].bitcast(F32).rearrange("p c (t j) -> p t c j", t=2),
                                  ALU.subtract).then_inc(xt_lo, 1)

            def split(parts, raw, done, count):
                dve.tensor_copy(parts[:, 0], raw).then_inc(split_hi, 1)
                dve.wait_ge(split_hi, count)
                dve.tensor_tensor(parts[:, 1], raw, parts[:, 0].bitcast(F32), ALU.subtract).then_inc(done, 1)

            def steps(plan, kind, hh, g, h):
                for what, which, nxt in plan:
                    if what == "WO":
                        dve.wait_ge(wo_loaded, (hh + 1) * 16)
                        if not (isinstance(hh, int) and hh == 0):
                            dve.wait_ge(r_banked, hh * ADDS + 1)
                        split(wo, wo_raw[:, :], wo_split, 2 * hh + 2 * (g + 1) + 2)
                    elif what == "WQ":
                        if kind == "last":
                            continue
                        hn = hh + nxt
                        dve.wait_ge(wq_loaded, (hn + 1) * 16)
                        if nxt:
                            dve.wait_ge(x_banked, chunk_at("next", "Q", BLOCKS - 1, g, h, 0) + 1)
                        split(wq, wq_raw[:, :, :], wq_split, 2 * hh + 2 * (g + 1) + 3 if nxt else 2)
                    elif what == "WKV":
                        gg = g + nxt
                        k = 0 if which[0] == "K" else 1
                        dve.wait_ge(wkv_loaded, (2 * gg + k + 1) * 16)
                        if k:
                            dve.wait_ge(x_banked, gg * XG + BLOCKS)
                        elif nxt:
                            dve.wait_ge(v_banked, gg * BLOCKS)
                        n = (1 if k == 0 else 3) if not nxt else 2 * (hh + 1) + 1 + 2 * gg + k + 1
                        split(wkv, wkv_raw[:, :, :], wkv_split, n)
                    elif what == "X":
                        n = chunk_at(kind, which[0], which[1], g, h, nxt)
                        r = which[1] % 2
                        cs = slice(which[1] * BW, (which[1] + 1) * BW)
                        dve.wait_ge(x_lo, n + 1)
                        dve.wait_ge(x_swapped, 2 * (n + 1))
                        dve.tensor_tensor(turned[:, r, :], s_bank[which[1]][:, :], cos[:, cs], ALU.mult).then_inc(x_cos, 1)
                    elif what == "Y":
                        n = chunk_at(kind, which[0], which[1], g, h, nxt)
                        dst = kt if which[0] == "K" else qt
                        cs = slice(which[1] * BW, (which[1] + 1) * BW)
                        dve.wait_ge(x_hi, n + 3)
                        dve.tensor_tensor(dst[:, 1, cs], turned[:, which[1] % 2, :], dst[:, 0, cs].bitcast(F32),
                                          ALU.subtract).then_inc(x_lo, 1)
                    elif what == "XV":
                        ch, = which
                        dve.wait_ge(v_hi, (g + nxt) * BLOCKS + ch + 1)
                        dve.tensor_tensor(vv[:, 1, ch * NB:(ch + 1) * NB, :], s_bank[ch][:, :].rearrange("p (t d) -> p t d", t=NB),
                                          vv[:, 0, ch * NB:(ch + 1) * NB, :].bitcast(F32), ALU.subtract).then_inc(v_lo, 1)
                    elif what == "S":
                        a, = which
                        st = a % STATS
                        n = a // NB + 1
                        first = (hh + nxt) * CHUNKS + chunk_no(a, 0)
                        for ch in range(n):
                            width = min(BW, (a + 1) * P - ch * BW)
                            dve.wait_ge(s_banked, first + ch + 1)
                            out = row_max[:, st, ch:ch + 1] if n > 1 else neg_max[:, st:st + 1]
                            ins = dve.tensor_reduce(out, s_bank[ch][:, 0:width], AX, ALU.max, negate=n == 1)
                            ins.then_inc(max_part if n > 1 else max_ready, 1)
                        if n > 1:
                            dve.wait_ge(max_part, (hh + nxt) * (CHUNKS - NB) + chunk_no(a, 0) - NB + n)
                            dve.tensor_reduce(neg_max[:, st:st + 1], row_max[:, st, 0:n], AX, ALU.max, negate=True)\
                               .then_inc(max_ready, 1)
                    elif what == "N":
                        a, = which
                        st = a % STATS
                        n = a // NB + 1
                        row = (hh + nxt) * ROWS + a
                        dve.wait_ge(exp_done, (hh + nxt) * CHUNKS + chunk_no(a, n - 1) + 1)
                        if n > 1:
                            dve.tensor_reduce(row_sum[:, st, 0:1], row_sum[:, st, 0:n], AX, ALU.add).then_inc(sum_part, 1)
                            dve.wait_ge(sum_part, (hh + nxt) * (ROWS - NB) + a - NB + 1)
                        dve.reciprocal(inv_sum[:, st:st + 1], row_sum[:, st, 0:1]).then_inc(inv_ready, 1)
                    elif what == "T":
                        i, j = which
                        slot = item_no(i, j) % SLOTS
                        c0 = max(j - NB * i, 0) * P
                        dve.wait_ge(t_hi, hh * ITEMS + item_no(i, j) + 1)
                        dve.tensor_tensor(pt[:, slot, 1, c0:], t_bank[bank_of(kind, (what, which))][:, c0:],
                                          pt[:, slot, 0, c0:].bitcast(F32), ALU.subtract).then_inc(t_lo, 1)
                    elif what == "O":
                        dve.wait_ge(o_hi, hh * BLOCKS + which[0] + 1)
                        dve.tensor_tensor(ot[:, 1, :], o_bank[:, :], ot[:, 0, :].bitcast(F32), ALU.subtract).then_inc(o_lo, 1)
                    elif what == "R":
                        i, half = which
                        bank = t_bank[bank_of(kind, (what, which))]
                        tt = i * NB + half * 2
                        dve.wait_ge(r_banked, hh * ADDS + 2 * i + half + 2)
                        dve.tensor_tensor(x[:, tt:tt + 2, :], bank[:, :].rearrange("p (t m) -> p t m", t=2),
                                          x[:, tt:tt + 2, :], ALU.add).then_inc(r_added, 1)

            walk(dve, steps)


def program(nc, x_in, w_aq, w_ak, w_av, w_ao, w_cls, bias, w_gate_up, w_down, cos, sin, out):
    with ExitStack() as ctx:
        c = constants(nc, ctx)
        x = ctx.enter_context(nc.sbuf_tensor("x", [P, NT, M], F32))
        wf = {"cls": w_cls, "bias": bias, "gate_up": w_gate_up, "down": w_down}
        wa = {"q": w_aq, "k": w_ak, "v": w_av, "o": w_ao}
        ffn(nc, "ffn1", c, x, x_in[0], wf, None)
        attention(nc, c, x, wa, cos, sin)
        ffn(nc, "ffn2", c, x, None, wf, out[0])


_INS = ["L0_attn_x", "L0_attn_w_aq", "L0_attn_w_ak", "L0_attn_w_av", "L0_attn_w_ao",
        "L0_ffn_w_cls", "L0_ffn_bias", "L0_ffn_w_gate_up", "L0_ffn_w_down"]
_OUTS = [((1, T, M), "float32")]


def rotation_tables():
    half = D // 2
    freqs = np.power(np.float32(10000.0), -np.arange(half, dtype=np.float32) / np.float32(half)).astype(np.float32)
    angles = (np.arange(T, dtype=np.float32)[:, None] * freqs[None, :]).astype(np.float64)
    scale = D ** -0.25
    cos, sin = np.cos(angles).T * scale, np.sin(angles).T * scale
    return (np.ascontiguousarray(np.concatenate([cos, cos]).astype(np.float32)),
            np.ascontiguousarray(np.concatenate([-sin, sin]).astype(np.float32)))


def kernel(**inputs):
    import numpy as _np
    import concourse.bacc as _bacc
    from concourse import mybir as _mybir
    from concourse.bass_utils import run_bass_kernel_spmd as _run

    nc = _bacc.Bacc("TRN2", target_bir_lowering=False, num_devices=1)
    arrays, args = {}, []
    cos, sin = rotation_tables()
    laid = {**{name: inputs[name] for name in _INS}, "cos": cos, "sin": sin}
    for name, a in laid.items():
        a = _np.ascontiguousarray(a)
        arrays[f"in_{name}_dram"] = a
        args.append(nc.dram_tensor(f"in_{name}_dram", a.shape, _mybir.dt.from_np(a.dtype), kind="ExternalInput").ap())
    for i, (shape, dtype) in enumerate(_OUTS):
        dt = _mybir.dt.from_np(_np.dtype(dtype))
        args.append(nc.dram_tensor(f"out_{i}_dram", shape, dt, kind="ExternalOutput").ap())
    program(nc, *args)
    r = _run(nc, [arrays], core_ids=[0])
    return r.results[0]["out_0_dram"]
```

```python
from contextlib import ExitStack

import numpy as np

import concourse.bass as bass
from concourse import mybir

F32 = mybir.dt.float32
F32R = mybir.dt.float32r
F16 = mybir.dt.float16
BF16 = mybir.dt.bfloat16
I32 = mybir.dt.int32
U32 = mybir.dt.uint32
ALU = mybir.AluOpType
ACT = mybir.ActivationFunctionType
AX = mybir.AxisListType.X

P = 128
T, M = 2048, 256
NT = T // P
MC = M // P
E, Z, K, CAP = 32, 32, 8, 128
EZ = E + Z
FF = 128
G, H, D = 4, 4, 128
SLOT_SUB = 8
SLOT_HI = CAP // SLOT_SUB
EG = P // SLOT_HI
NG = E // EG
LO_SCALE = 2048.0
EARLY = 4
PAIR = 2
RING = 4
EPS_LN, EPS_W, SCALE_W = 1e-5, 1e-20, 1.5
NOT_CHOSEN = 1000.0


class Steps:

    def __init__(self, eng, sem):
        self.eng, self.sem, self.n = eng, sem, 0

    def __call__(self, ins):
        ins.then_inc(self.sem, 1)
        self.n += 1

    def done(self):
        self.eng.wait_ge(self.sem, self.n)


def constants(nc, ctx):
    def sb(name, shape, dt):
        return ctx.enter_context(nc.sbuf_tensor(name, shape, dt))

    c = {}
    c["ident"] = ident = sb("ident", [P, P], F32)
    c["ident16"] = ident16 = sb("ident16", [P, P], BF16)
    c["before"] = before = sb("before", [P, P], BF16)
    c["ones16"] = ones16 = sb("ones16", [P, P], BF16)
    c["future"] = future = sb("future", [P, P], BF16)
    c["iota_hi"] = iota_hi = sb("iota_hi", [P, SLOT_HI], F16)
    c["iota_lo"] = iota_lo = sb("iota_lo", [P, SLOT_SUB], F16)
    c["token"] = token = sb("token", [P, NT, EG], F16)
    c["own"] = own = sb("own", [P, EG], F32)
    made = ctx.enter_context(nc.semaphore("const_made"))
    with nc.Block() as block:

        @block.gpsimd
        def _(pool):
            step = Steps(pool, made)
            step(pool.memset(ident[:, :], 0.0))
            step(pool.memset(ident16[:, :], 0.0))
            step(pool.memset(before[:, :], 1.0))
            step(pool.memset(future[:, :], 0.0))
            step(pool.memset(own[:, :], 1.0))
            step(pool.memset(ones16[:, :], 1.0))
            step(pool.iota(iota_hi[:, :], [[1, SLOT_HI]], base=0, channel_multiplier=0,
                           allow_small_or_imprecise_dtypes=True))
            step(pool.iota(iota_lo[:, :], [[1, SLOT_SUB]], base=0, channel_multiplier=0,
                           allow_small_or_imprecise_dtypes=True))
            step(pool.iota(token[:, :, :], [[P, NT], [0, EG]], base=0, channel_multiplier=1,
                           allow_small_or_imprecise_dtypes=True))
            step.done()
            for t in (ident, ident16):
                step(pool.affine_select(out=t[:, :], in_=t[:, :], compare_op=ALU.not_equal, fill=1.0,
                                        base=0, pattern=[[-1, P]], channel_multiplier=1))
            step(pool.affine_select(out=before[:, :], in_=before[:, :], compare_op=ALU.is_gt, fill=0.0,
                                    base=0, pattern=[[1, P]], channel_multiplier=-1))
            step(pool.affine_select(out=future[:, :], in_=future[:, :], compare_op=ALU.is_ge, fill=-1e30,
                                    base=0, pattern=[[-1, P]], channel_multiplier=1))
            step(pool.affine_select(out=own[:, :], in_=own[:, :], compare_op=ALU.is_ge, fill=0.0,
                                    base=0, pattern=[[-SLOT_HI, EG]], channel_multiplier=1))
            step.done()
            step(pool.affine_select(out=own[:, :], in_=own[:, :], compare_op=ALU.is_ge, fill=0.0,
                                    base=SLOT_HI - 1, pattern=[[SLOT_HI, EG]], channel_multiplier=-1))
            step.done()
    return c


def layernorm(dve, v, x, x_loaded, stats, mv, small, var_ready, root_done, xn, xn_ready):
    for t in range(NT):
        if x_loaded is not None and t % (NT // 4) == 0:
            dve.wait_ge(x_loaded[t // (NT // 4)], 16)
        v(dve.bn_stats(stats[:, t, :], x[:, t, :]))
    v.done()
    for t in range(NT):
        v(dve.bn_aggr(mv[:, t, :], stats[:, t, :]))
    v.done()
    var, root, inv, tmp = (small[:, i, :] for i in range(4))
    dve.tensor_scalar(var, mv[:, :, 1], EPS_LN, None, ALU.add).then_inc(var_ready, 1)
    dve.wait_ge(root_done, 1)
    v(dve.reciprocal(inv, root))
    v.done()
    v(dve.tensor_tensor(tmp, inv, inv, ALU.mult))
    v.done()
    v(dve.tensor_tensor(tmp, tmp, var, ALU.mult))
    v.done()
    v(dve.tensor_scalar(tmp, tmp, -0.5, 1.5, ALU.mult, ALU.add))
    v.done()
    v(dve.tensor_tensor(inv, inv, tmp, ALU.mult))
    v.done()
    for t in range(NT):
        ins = dve.tensor_scalar(xn[:, t, :], x[:, t, :], mv[:, t, 0:1], inv[:, t:t + 1],
                                ALU.subtract, ALU.mult)
        if t % (NT // 4) == NT // 4 - 1:
            ins.then_inc(xn_ready, 1)


def ffn(nc, n, c, x, x_dram, w, out):
    top = ExitStack()

    def sb(name, shape, dt, ctx=top):
        return ctx.enter_context(nc.sbuf_tensor(f"{n}_{name}", shape, dt))

    def sem(name):
        return top.enter_context(nc.semaphore(f"{n}_{name}"))

    xn_dram = nc.dram_tensor(f"{n}_xn_dram", (T, M), F32, kind="Internal").ap()
    table_dram = nc.dram_tensor(f"{n}_table_dram", (2, E * CAP), F32, kind="Internal").ap()

    with top:
        psum = [top.enter_context(nc.psum_tensor(f"{n}_bank{i}", [P, 512], F32)) for i in range(2)]
        lg = top.enter_context(nc.psum_tensor(f"{n}_lg", [P, NT, EZ], F32))
        psum += [None, None]
        psum += [top.enter_context(nc.psum_tensor(f"{n}_bank{i}", [P, 512], F32)) for i in range(4, 8)]
        gu_bank = [psum[6], psum[7]]
        y_bank = [psum[4], psum[5]]
        sum_bank = [psum[0:2], psum[4:6]]
        early_sum = lg[:, :, :].rearrange("p t e -> p (t e)").rearrange("p (t m) -> p t m", t=EARLY)

        tok = sb("tok", [P, E], F32)
        tok_index = sb("tok_index", [P, E], U32)
        slot_w = sb("slot_w", [P, E], F32)
        wgu = sb("wgu", [P, RING, MC, 2 * FF], F32)
        wd = sb("wd", [P, RING, M], F32)
        rows = sb("rows", [P, RING, M], F32)
        rows_t = sb("rows_t", [P, 2, MC, CAP], F32)
        gate = sb("gate", [P, 2, CAP], F32)
        act_t = sb("act_t", [P, 2, CAP], F32)

        iota_t = sb("iota_t", [P, T], F16)
        zeros16 = sb("zeros16", [P, 512], BF16)

        early = ExitStack()
        wcls_raw = sb("wcls_raw", [EZ, M], F32, early)
        wcls_t = sb("wcls_t", [P, MC, EZ], F32, early)
        bias = sb("bias", [P, EZ], F32, early)
        stats = sb("stats", [P, NT, 6], F32, early)
        mv = sb("mv", [P, NT, 2], F32, early)
        small = sb("small", [P, 8, NT], F32, early)
        xn = sb("xn", [P, NT, M], F32, early)
        xn_t = sb("xn_t", [P, MC, T], F32, early)
        score = sb("score", [P, NT, EZ], F32, early)
        biased = sb("biased", [P, NT, EZ], F32, early)
        left = sb("left", [P, NT, EZ], F32, early)
        top8 = sb("top8", [P, NT, K], F32, early)
        mask = sb("mask", [P, NT, EZ], F32, early)
        mask16 = sb("mask16", [P, NT, E], BF16, early)
        unchosen = sb("unchosen", [P, NT, E], F32, early)
        weight = sb("weight", [P, NT, E], F32, early)
        w_hi = sb("w_hi", [P, NT, E], F16, early)
        w_lo = sb("w_lo", [P, NT, E], F16, early)
        pos = sb("pos", [P, NT, E], I32, early)
        part = sb("part", [P, 2, NT, E], I32, early)
        part16 = sb("part16", [P, 2, NT, E], F16, early)
        hot_hi = sb("hot_hi", [P, NT, E, SLOT_HI], F16, early)
        hot_lo = sb("hot_lo", [P, NT, E, SLOT_SUB], F16, early)
        vals = sb("vals", [P, NT, NG, 3, EG * SLOT_SUB], F16, early)
        picked = sb("picked", [P, NG, 3, SLOT_SUB, EG], F32, early)
        summed = sb("summed", [P, NG, 3, SLOT_SUB], F32, early)
        table = sb("table", [P, 2, NG, SLOT_SUB], F32, early)
        table_es = sb("table_es", [2 * E, CAP], F32, early)
        early.close()
        y = sb("y", [P, E, 2, M], F32R)
        hot = sb("hot", [P, 2, E, PAIR * P], F32R)
        hot_early = sb("hot_early", [P, 2, EARLY * P], F32R)

        x_loaded = [sem(f"x_loaded{q}") for q in range(4)]
        w_loaded, step_v, var_ready, root_done = map(sem, ("w_loaded", "step_v", "var_ready", "root_done"))
        xn_ready, xn_stored, xt_banked, xt_copied = map(sem, ("xn_ready", "xn_stored", "xt_banked", "xt_copied"))
        cls_banked, cls_copied, logits_ready, shifted, exp_done = map(sem, ("cls_banked", "cls_copied", "logits_ready", "shifted", "exp_done"))
        mask_ready, pos_ready, vals_ready, picked_ready, table_ready = map(sem, ("mask_ready", "pos_ready", "vals_ready", "picked_ready", "table_ready"))
        table_stored, table_loaded, slots_banked, slots_ready = map(sem, ("table_stored", "table_loaded", "slots_banked", "slots_ready"))
        gathered = [sem(f"gathered{i}") for i in range(RING)]
        fetched = [sem(f"fetched{i}") for i in range(RING)]
        rt_banked, rt_copied, gu_banked, silu_done, act_ready, y_banked, hi_done, lo_done = map(
            sem, ("rt_banked", "rt_copied", "gu_banked", "silu_done", "act_ready", "y_banked", "hi_done", "lo_done"))
        iota_made, hot_ready, sum_banked, half_added, stored = map(sem, ("iota_made", "hot_ready", "sum_banked", "half_added", "stored"))
        hot_early_ready, early_done, early_added = map(sem, ("hot_early_ready", "early_done", "early_added"))
        step_p, factor_ready, hot_lo_ready, group_ready = map(sem, ("step_p", "factor_ready", "hot_lo_ready", "group_ready"))
        PAIRS = (NT - EARLY) // PAIR
        HOT_PARTS = 4
        BODY = RING
        HEAD = 4
        PASSES = (E - 1 - HEAD) // BODY

        def expert_steps(eng, first, step):
            first()
            for e in range(HEAD):
                step(e, e)
            with eng.Fori(0, PASSES) as i:
                for k in range(HEAD, HEAD + BODY):
                    step(i * BODY + k, k)
            for e in range(PASSES * BODY + HEAD, E + 1):
                step(e, e % RING)

        block = top.enter_context(nc.Block())

        @block.sync
        def _(sp):
            if x_dram is not None:
                for q in range(4):
                    ts = slice(q * NT // 4, (q + 1) * NT // 4)
                    sp.dma_start(x[:, ts, :], x_dram.rearrange("(t p) m -> p t m", p=P)[:, ts, :]).then_inc(x_loaded[q], 16)
            sp.dma_start(wcls_raw[:, :], w["cls"]).then_inc(w_loaded, 16)
            sp.dma_start(bias[:, :], w["bias"].rearrange("(a n) -> a n", a=1).to_broadcast([P, EZ])).then_inc(w_loaded, 16)

            def fetch(e, k):
                sp.dma_start(wgu[:, k % RING], w["gate_up"][e].rearrange("(c p) f -> p c f", p=P)).then_inc(fetched[k % RING], 16)
                sp.dma_start(wd[:, k % RING], w["down"][e]).then_inc(fetched[k % RING], 16)

            for e in range(RING):
                fetch(e, e)
            for q in range(4):
                ts = slice(q * NT // 4, (q + 1) * NT // 4)
                sp.wait_ge(xn_ready, q + 1)
                sp.dma_start(xn_dram.rearrange("(t p) m -> p t m", p=P)[:, ts, :], xn[:, ts, :]).then_inc(xn_stored, 16)
            sp.wait_ge(table_ready, 1)
            for v in range(2):
                sp.dma_start(table_dram[v].rearrange("(g p b) -> p g b", g=NG, p=P), table[:, v]).then_inc(table_stored, 16)
            sp.wait_ge(table_stored, 32)
            sp.dma_start(table_es[:, :], table_dram.rearrange("v (e s) -> (v e) s", e=E)).then_inc(table_loaded, 16)
            with sp.Fori(1, E // RING) as i:
                for k in range(RING):
                    sp.wait_ge(y_banked, (i - 1) * RING + k + 1)
                    fetch(i * RING + k, k)
            if out is not None:
                for t in range(0, NT, 2):
                    if t < EARLY:
                        sp.wait_ge(early_added, t // 2 + 1)
                    else:
                        sp.wait_ge(half_added, 8 + 2 * (t + 2 - EARLY))
                    sp.dma_start(out.rearrange("(t p) m -> p t m", p=P)[:, t:t + 2, :], x[:, t:t + 2, :]).then_inc(stored, 16)
                sp.wait_ge(stored, NT // 2 * 16)

        @block.gpsimd
        def _(pool):
            p = Steps(pool, step_p)
            pool.iota(iota_t[:, :], [[1, T]], base=0, channel_multiplier=0,
                      allow_small_or_imprecise_dtypes=True).then_inc(iota_made, 1)
            pool.memset(zeros16[:, :], 0.0).then_inc(iota_made, 1)
            pool.wait_ge(factor_ready, 1)
            p(pool.tensor_tensor(weight[:, :, :], score[:, :, 0:E], small[:, 7, :].unsqueeze(2).to_broadcast([P, NT, E]), ALU.mult))
            p.done()
            p(pool.tensor_copy(w_hi[:, :, :], weight[:, :, :]))
            p.done()
            p(pool.tensor_tensor(weight[:, :, :], weight[:, :, :], w_hi[:, :, :], ALU.subtract))
            p.done()
            p(pool.tensor_scalar(w_lo[:, :, :], weight[:, :, :], LO_SCALE, None, ALU.mult))
            p.done()
            pool.wait_ge(hot_lo_ready, 1)
            for g in range(NG):
                es = slice(g * EG, (g + 1) * EG)
                for i, half in enumerate((w_hi, w_lo)):
                    pool.tensor_tensor(vals[:, :, g, 1 + i, :].rearrange("p t (e b) -> p t e b", e=EG), hot_lo[:, :, es, :],
                                       half[:, :, es].unsqueeze(3).to_broadcast([P, NT, EG, SLOT_SUB]),
                                       ALU.mult).then_inc(vals_ready, 1)
            pool.wait_ge(xn_stored, 64)
            pool.wait_ge(slots_ready, 1)

            for e in range(E):
                if e >= RING:
                    pool.wait_ge(rt_banked, e - RING + 1)
                pool.indirect_dma_start(
                    out=rows[:, e % RING, :], out_offset=None, in_=xn_dram,
                    in_offset=bass.IndirectOffsetOnAxis(tok_index[:, e:e + 1], 0)).then_inc(gathered[e % RING], 16)

        @block.scalar
        def _(act):
            act.wait_ge(var_ready, 1)
            nc.scalar.activation(small[:, 1, :], small[:, 0, :], ACT.Sqrt).then_inc(root_done, 1)
            act.wait_ge(cls_banked, 1)
            nc.scalar.activation(wcls_t[:, :, :], lg[:, 0:2 * MC // 2, :], ACT.Copy).then_inc(cls_copied, 1)
            for q in range(NT // 2):
                act.wait_ge(xt_banked, q + 1)
                nc.scalar.activation(
                    xn_t[:, :, q * 2 * P:(q + 1) * 2 * P].rearrange("p c (t j) -> p t c j", t=2),
                    psum[q % 2][:, :].rearrange("p (t c j) -> p t c j", t=2, c=MC), ACT.Copy).then_inc(xt_copied, 1)
            act.wait_ge(shifted, 1)
            nc.scalar.activation(score[:, :, :], biased[:, :, :], ACT.Exp).then_inc(exp_done, 1)

            def step(e, k):
                if not (isinstance(e, int) and e == E):
                    act.wait_ge(gu_banked, e + 1)
                    nc.scalar.activation(gate[:, k % 2, :], gu_bank[k % 2][:, 0:CAP], ACT.Silu).then_inc(silu_done, 1)
                if not (isinstance(e, int) and e == 0):
                    act.wait_ge(y_banked, e)
                    nc.scalar.activation(y[:, bass.ds(e - 1, 1), 0, :], y_bank[(k - 1) % 2][:, 0:M], ACT.Copy,
                                         scale=slot_w[:, bass.ds(e - 1, 1)]).then_inc(hi_done, 1)

            act.wait_ge(slots_ready, 1)
            expert_steps(act, lambda: None, step)

        @block.tensor
        def _(pe):
            pe.wait_ge(w_loaded, 32)
            for ch in range(MC):
                ins = pe.transpose(lg[:, ch, :], wcls_raw[:, ch * P:(ch + 1) * P], c["ident"][0:EZ, 0:EZ])
            ins.then_inc(cls_banked, 1)
            for q in range(NT // 2):
                pe.wait_ge(xn_ready, q // 2 + 1)
                if q >= 2:
                    pe.wait_ge(xt_copied, q - 1)
                for t in range(2):
                    for ch in range(MC):
                        ins = pe.transpose(psum[q % 2][:, (t * MC + ch) * P:(t * MC + ch + 1) * P],
                                           xn[:, 2 * q + t, ch * P:(ch + 1) * P], c["ident"][:, :])
                ins.then_inc(xt_banked, 1)
            pe.wait_ge(cls_copied, 1)
            for t in range(NT):
                pe.wait_ge(xt_copied, t // 2 + 1)
                for ch in range(MC):
                    ins = pe.matmul(lg[:, t, :], xn_t[:, ch, t * P:(t + 1) * P], wcls_t[:, ch, :],
                                    start=ch == 0, stop=ch == MC - 1)
            ins.then_inc(logits_ready, 1)
            pe.wait_ge(mask_ready, 1)
            rank = psum[4][:, :].rearrange("p (t e) -> p t e", t=NT)
            pe.matmul(rank, c["before"][:, :], mask16[:, :, :], start=True, stop=False, skip_group_check=True)
            for t in range(NT - 1):
                ins = pe.matmul(rank[:, t + 1:, :], c["ones16"][:, :],
                                mask16[:, t:t + 1, :].to_broadcast([P, NT - 1 - t, E]),
                                start=False, stop=t == NT - 2, skip_group_check=True)
            ins.then_inc(pos_ready, 1)
            for g in range(NG):
                pe.wait_ge(group_ready, 2 * g + 2)
                pe.wait_ge(vals_ready, 2 * g + 2)
                for t in range(NT):
                    ins = pe.matmul(psum[5 + g // 2][:, (g % 2) * 256:(g % 2) * 256 + 3 * EG * SLOT_SUB],
                                    hot_hi[:, t, g * EG:(g + 1) * EG, :].rearrange("p e a -> p (e a)"),
                                    vals[:, t, g].rearrange("p v n -> p (v n)"),
                                    start=t == 0, stop=t == NT - 1)
            ins.then_inc(picked_ready, 1)
            pe.wait_ge(table_loaded, 16)
            pe.transpose(psum[4][:, 0:2 * E], table_es[:, :], c["ident"][0:2 * E, 0:2 * E]).then_inc(slots_banked, 1)

            def turn(e, k):
                pe.wait_ge(gathered[k % RING], 16 * (e // RING + 1))
                if isinstance(e, int) and e < 2:
                    pass
                else:
                    pe.wait_ge(rt_copied, e - 1)
                for ch in range(MC):
                    ins = pe.transpose(psum[k % 2][:, ch * P:(ch + 1) * P], rows[:, k % RING, ch * P:(ch + 1) * P],
                                       c["ident"][:, :])
                ins.then_inc(rt_banked, 1)

            def combine_early(e, k):
                pe.wait_ge(lo_done, e + 3)
                pe.wait_ge(hot_early_ready, e + 1)
                last = isinstance(e, int) and e == E - 1
                for t in range(EARLY):
                    for half in range(2):
                        ins = pe.matmul(early_sum[:, t, :], hot_early[:, k % 2, t * P:(t + 1) * P],
                                        y[:, bass.ds(e, 1), half, :], start=False,
                                        stop=last and half == 1, skip_group_check=True)
                ins.then_inc(early_done, 1)

            def step(e, k):
                last = isinstance(e, int) and e >= E
                if not last:
                    pe.wait_ge(fetched[k % RING], 32 * (e // RING + 1))
                    pe.wait_ge(rt_copied, e + 1)
                    if not (isinstance(e, int) and e < 2):
                        pe.wait_ge(act_ready, e - 1)
                    for half in range(2):
                        for ch in range(MC):
                            ins = pe.matmul(gu_bank[k % 2][:, half * CAP:(half + 1) * CAP],
                                            wgu[:, k % RING, ch, half * FF:(half + 1) * FF], rows_t[:, k % 2, ch, :],
                                            start=ch == 0, stop=ch == MC - 1)
                    ins.then_inc(gu_banked, 1)
                if not (isinstance(e, int) and e >= E - 1):
                    turn(e + 1, k + 1)
                if not (isinstance(e, int) and e == 0):
                    pe.wait_ge(act_ready, e)
                    pe.wait_ge(lo_done, e)
                    pe.matmul(y_bank[(k - 1) % 2][:, 0:M], act_t[:, (k - 1) % 2, :], wd[:, (k - 1) % RING, :],
                              start=True, stop=True).then_inc(y_banked, 1)
                if not (isinstance(e, int) and e < 2):
                    combine_early(e - 2, k - 2)

            pe.wait_ge(iota_made, 2)
            for b in range(EARLY // 2):
                pe.matmul(lg[:, b * NT // 2:(b + 1) * NT // 2, :], c["ones16"][:, :], zeros16[:, :],
                          start=True, stop=False, skip_group_check=True)
            expert_steps(pe, lambda: turn(0, 0), step)
            combine_early(E - 1, E - 1)

            with pe.Fori(0, PAIRS // 2) as i:
                for k in range(2):
                    pair = i * 2 + k
                    pe.wait_ge(half_added, 2 * PAIR * pair + 4)
                    for t in range(PAIR):
                        for e in range(E):
                            if t == 0 and e % (E // HOT_PARTS) == 0:
                                pe.wait_ge(hot_ready, pair * HOT_PARTS + e // (E // HOT_PARTS) + 1)
                            ins = pe.matmul(sum_bank[k][t][:, :], hot[:, k, e, t * P:(t + 1) * P],
                                            y[:, e].rearrange("p h m -> p (h m)"), start=e == 0, stop=e == E - 1)
                        ins.then_inc(sum_banked, 1)

        @block.vector
        def _(dve):
            v = Steps(dve, step_v)
            dve.engine_nop().then_inc(lo_done, 2)
            dve.engine_nop().then_inc(early_done, 2)
            layernorm(dve, v, x, None if x_dram is None else x_loaded, stats, mv, small, var_ready, root_done, xn, xn_ready)
            dve.wait_ge(logits_ready, 1)
            big, den, chosen, zero_w = (small[:, i, :] for i in range(4, 8))

            def over(a, width=EZ):
                return a.unsqueeze(2).to_broadcast([P, NT, width])

            v(dve.tensor_reduce(big, lg[:, :, :], AX, ALU.max))
            v.done()
            dve.tensor_tensor(biased[:, :, :], lg[:, :, :], over(big), ALU.subtract).then_inc(shifted, 1)
            dve.wait_ge(exp_done, 1)
            v(dve.tensor_reduce(den, score[:, :, :], AX, ALU.add))
            v.done()
            v(dve.reciprocal(den, den))
            v.done()
            v(dve.tensor_tensor(score[:, :, :], score[:, :, :], over(den), ALU.mult))
            v.done()
            v(dve.tensor_tensor(biased[:, :, :], score[:, :, :],
                                bias[:, :].unsqueeze(1).to_broadcast([P, NT, EZ]), ALU.add))
            v.done()
            for t in range(NT):
                v(dve.max(top8[:, t, :], biased[:, t, :]))
            v.done()
            for t in range(NT):
                v(dve.match_replace(left[:, t, :], top8[:, t, :], biased[:, t, :], -3e38))
            v.done()
            v(dve.tensor_tensor(mask[:, :, :], biased[:, :, :], left[:, :, :], ALU.not_equal))
            v.done()
            dve.tensor_copy(mask16[:, :, :], mask[:, :, 0:E]).then_inc(mask_ready, 1)
            v(dve.tensor_scalar(unchosen[:, :, :], mask[:, :, 0:E], -NOT_CHOSEN, NOT_CHOSEN, ALU.mult, ALU.add))
            v(dve.tensor_tensor(score[:, :, :], score[:, :, :], mask[:, :, :], ALU.mult))
            v.done()
            v(dve.tensor_reduce(chosen, score[:, :, :], AX, ALU.add))
            v(dve.tensor_reduce(zero_w, score[:, :, E:EZ], AX, ALU.add))
            v.done()
            v(dve.tensor_scalar(chosen, chosen, EPS_W, None, ALU.add))
            v.done()
            v(dve.reciprocal(chosen, chosen))
            v.done()
            v(dve.tensor_scalar(chosen, chosen, SCALE_W, None, ALU.mult))
            v.done()
            v(dve.tensor_tensor(zero_w, zero_w, chosen, ALU.mult))
            v.done()
            v(dve.scalar_tensor_tensor(zero_w, zero_w, 1.0, chosen, ALU.add, ALU.mult))
            v.done()
            dve.engine_nop().then_inc(factor_ready, 1)
            dve.wait_ge(pos_ready, 1)
            v(dve.tensor_tensor(pos[:, :, :], psum[4][:, :].rearrange("p (t e) -> p t e", t=NT),
                                unchosen[:, :, :], ALU.add))
            v.done()
            v(dve.tensor_scalar(part[:, 0], pos[:, :, :], SLOT_SUB.bit_length() - 1, None, ALU.arith_shift_right))
            v(dve.tensor_scalar(part[:, 1], pos[:, :, :], SLOT_SUB - 1, None, ALU.bitwise_and))
            v.done()
            v(dve.tensor_copy(part16[:, :, :, :], part[:, :, :, :]))
            v.done()
            v(dve.tensor_tensor(hot_lo[:, :, :, :].rearrange("p t e b -> p (t e) b"),
                                part16[:, 1].rearrange("p t e -> p (t e)").unsqueeze(2).to_broadcast([P, NT * E, SLOT_SUB]),
                                c["iota_lo"][:, :].unsqueeze(1).to_broadcast([P, NT * E, SLOT_SUB]), ALU.is_equal))
            v.done()
            dve.engine_nop().then_inc(hot_lo_ready, 1)
            for g in range(NG):
                es = slice(g * EG, (g + 1) * EG)
                dve.tensor_tensor(hot_hi[:, :, es, :], part16[:, 0, :, es].unsqueeze(3).to_broadcast([P, NT, EG, SLOT_HI]),
                                  c["iota_hi"][:, :].unsqueeze(1).unsqueeze(1).to_broadcast([P, NT, EG, SLOT_HI]),
                                  ALU.is_equal).then_inc(group_ready, 1)
                dve.tensor_tensor(vals[:, :, g, 0, :].rearrange("p t (e b) -> p t e b", e=EG), hot_lo[:, :, es, :],
                                  c["token"][:, :, :].unsqueeze(3).to_broadcast([P, NT, EG, SLOT_SUB]),
                                  ALU.mult).then_inc(group_ready, 1)
            dve.wait_ge(picked_ready, 1)
            for g in range(NG):
                v(dve.tensor_tensor(
                    picked[:, g], psum[5 + g // 2][:, (g % 2) * 256:(g % 2) * 256 + 3 * EG * SLOT_SUB]
                    .rearrange("p (v e b) -> p v b e", v=3, e=EG),
                    c["own"][:, :].unsqueeze(1).unsqueeze(1).to_broadcast([P, 3, SLOT_SUB, EG]), ALU.mult))
            v.done()
            v(dve.tensor_reduce(summed[:, :, :, :], picked[:, :, :, :, :].rearrange("p g v b e -> p (g v b) e"), AX, ALU.add))
            v.done()
            v(dve.tensor_copy(table[:, 0], summed[:, :, 0, :]))
            v(dve.scalar_tensor_tensor(table[:, 1], summed[:, :, 2, :], 1.0 / LO_SCALE, summed[:, :, 1, :],
                                       ALU.mult, ALU.add))
            v.done()
            dve.engine_nop().then_inc(table_ready, 1)
            dve.wait_ge(slots_banked, 1)
            v(dve.tensor_copy(tok[:, :], psum[4][:, 0:E]))
            v(dve.tensor_copy(tok_index[:, :], psum[4][:, 0:E]))
            v(dve.tensor_copy(slot_w[:, :], psum[4][:, E:2 * E]))
            v.done()
            dve.engine_nop().then_inc(slots_ready, 1)

            def copy_rows(e, k):
                dve.wait_ge(rt_banked, e + 1)
                if not (isinstance(e, int) and e < 2):
                    dve.wait_ge(gu_banked, e - 1)
                dve.tensor_copy(rows_t[:, k % 2], psum[k % 2][:, 0:M].rearrange("p (c s) -> p c s", c=MC)).then_inc(rt_copied, 1)

            def step(e, k):
                if not (isinstance(e, int) and e >= E):
                    dve.wait_ge(silu_done, e + 1)
                    if not (isinstance(e, int) and e < 2):
                        dve.wait_ge(y_banked, e - 1)
                    dve.tensor_tensor(act_t[:, k % 2, :], gate[:, k % 2, :], gu_bank[k % 2][:, CAP:2 * CAP],
                                      ALU.mult).then_inc(act_ready, 1)
                if not (isinstance(e, int) and e >= E - 1):
                    copy_rows(e + 1, k + 1)
                if not (isinstance(e, int) and e == 0):
                    dve.wait_ge(hi_done, e)
                    dve.scalar_tensor_tensor(y[:, bass.ds(e - 1, 1), 1, :], y_bank[(k - 1) % 2][:, 0:M],
                                             slot_w[:, bass.ds(e - 1, 1)], y[:, bass.ds(e - 1, 1), 0, :].bitcast(F32),
                                             ALU.mult, ALU.subtract).then_inc(lo_done, 1)
                    dve.wait_ge(early_done, e)
                    dve.tensor_scalar(hot_early[:, (k - 1) % 2, :], iota_t[:, 0:EARLY * P], tok[:, bass.ds(e - 1, 1)], None,
                                      ALU.is_equal).then_inc(hot_early_ready, 1)

            dve.wait_ge(iota_made, 2)
            expert_steps(dve, lambda: copy_rows(0, 0), step)

            dve.engine_nop().then_inc(half_added, 8)
            PART = E // HOT_PARTS

            def make_hot(pair, k):
                for e in range(E):
                    ins = dve.tensor_scalar(hot[:, k, e, :], iota_t[:, bass.ds(EARLY * P + pair * PAIR * P, PAIR * P)],
                                            tok[:, e:e + 1], None, ALU.is_equal)
                    if e % PART == PART - 1:
                        ins.then_inc(hot_ready, 1)

            def add_sum(pair, k):
                for t in range(PAIR):
                    row = x[:, bass.ds(EARLY + pair * PAIR + t, 1), :]
                    dve.wait_ge(sum_banked, pair * PAIR + t + 1)
                    for half in (1, 0):
                        dve.scalar_tensor_tensor(row, sum_bank[k][t][:, half * M:(half + 1) * M], 0.5, row,
                                                 ALU.mult, ALU.add).then_inc(half_added, 1)
                        dve.wait_ge(half_added, 8 + 2 * (pair * PAIR + t) + (1 if half else 2))

            make_hot(0, 0)
            dve.wait_ge(early_done, E + 2)
            for b in range(EARLY // 2):
                rows2 = x[:, 2 * b:2 * b + 2, :]
                dve.scalar_tensor_tensor(rows2, early_sum[:, 2 * b:2 * b + 2, :], 0.5, rows2, ALU.mult, ALU.add).then_inc(early_added, 1)
            make_hot(1, 1)
            with dve.Fori(0, PAIRS // 2 - 1) as i:
                for k in range(2):
                    add_sum(i * 2 + k, k)
                    make_hot(i * 2 + k + 2, k)
            add_sum(PAIRS - 2, 0)
            add_sum(PAIRS - 1, 1)


NB = 4
BW = NB * P
BLOCKS = T // BW
CHUNKS = NB * BLOCKS * (BLOCKS + 1) // 2
ITEMS = CHUNKS
ADDS = 2 * BLOCKS
SLOTS = 3
FLUSH = 1
LAG = 2
ROWS = NB * BLOCKS


def cut(sizes, first=0):
    return [range(first + sum(sizes[:q]), first + sum(sizes[:q + 1])) for q in range(len(sizes))]


BESIDE = (1, 1, 2, 4)
BESIDE_EDGE = (2, 1, 1, 1, 2, 1, 1, 1, 2, 1, 1, 2)
GROUPS = [cut((1, 1, 1, 1)), cut((2, 2, 2, 2)), cut((3, 3, 3, 3)), cut((3, 3, 2, 0), sum(BESIDE))]
STATS = 8


def chunk_no(a, ch):
    return sum(r // NB + 1 for r in range(a)) + ch


def item_no(i, j):
    return NB * i * (i + 1) // 2 + j


def head_plan():
    plan = []
    waiting = {"E": [], "N": [], "V": []}

    def flush_exp(n):
        for _ in range(min(n, len(waiting["E"]))):
            plan.append(waiting["E"].pop(0))

    def scores(a, nxt=0):
        flush_exp(99)
        for ch in range(a // NB + 1):
            plan.append(("S", (a, ch), nxt))
            if a % NB == 0 and ch == FLUSH:
                value(len(waiting["V"]))
        while len(waiting["N"]) > 1:
            plan.append(waiting["N"].pop(0))
        waiting["E"] += [("E", (a, ch), nxt) for ch in range(a // NB + 1)]
        waiting["N"].append(("N", (a,), nxt))

    def value(n):
        for _ in range(n):
            v = waiting["V"].pop(0)
            plan.append(v)
            i, j = v[1]
            if j == NB * (i + 1) - 1:
                plan.append(("O", (i,), 0))

    def items(i, js):
        for m, j in enumerate(js):
            plan.append(("T", (i, j), 0))
            waiting["V"].append(("V", (i, j), 0))
            if len(waiting["V"]) > LAG:
                value(1)
            if waiting["E"]:
                flush_exp(1 if m else 0)
            elif len(waiting["N"]) > 1:
                plan.append(waiting["N"].pop(0))

    def output(i):
        plan.extend([("R", (i, 0), 0), ("R", (i, 1), 0)])

    for i in range(BLOCKS - 1):
        groups = GROUPS[i]
        for q in range(NB):
            scores(NB * (i + 1) + q)
            items(i, groups[q])
            if q == 1 and i:
                output(i - 1)
            if q == NB - 1 and i == 0:
                plan.append(("WO", (), 0))
            if q == 2 and i == 1:
                plan.append(("WQ", (), 1))
    body = list(plan)
    plan.clear()
    i, n = BLOCKS - 1, NB * BLOCKS
    saved = {k: list(v) for k, v in waiting.items()}

    def tail(kind):
        plan.clear()
        for k in waiting:
            waiting[k] = list(saved[k])
        flush_exp(99)
        if kind == "last":
            while waiting["N"]:
                plan.append(waiting["N"].pop(0))
            items(i, range(0, 6))
            output(i - 1)
            items(i, range(6, n))
            value(len(waiting["V"]))
            output(i)
            return list(plan)
        xs = [("Q", ch) for ch in range(BLOCKS)]
        beside = BESIDE
        if kind == "edge":
            xs = [("K", ch) for ch in range(BLOCKS)] + xs + [("U", ch) for ch in range(BLOCKS)]
            beside = BESIDE_EDGE
        before = None
        at = 0
        for m, x in enumerate(xs):
            if x == ("K", 0):
                plan.append(("WKV", ("K",), 1))
            if x == ("Q", 1) and kind == "edge":
                plan.append(("WKV", ("V",), 1))
            plan.append(("U", x[1:], 1) if x[0] == "U" else ("X", x, 1))
            if m == 0:
                value(len(waiting["V"]))
            while waiting["N"]:
                plan.append(waiting["N"].pop(0))
            items(i, range(at, at + beside[m]))
            at += beside[m]
            if m == 1:
                output(i - 1)
            if before:
                plan.append(("Y", before, 1))
            before = x if x[0] != "U" else None
        if before:
            plan.append(("Y", before, 1))
        if kind == "edge":
            assert at == n
            value(len(waiting["V"]))
            for ch in range(BLOCKS):
                plan.append(("XV", (ch,), 1))
            for q in range(NB):
                scores(q, 1)
            flush_exp(99)
        else:
            groups = GROUPS[i]
            for q in range(NB):
                scores(q, 1)
                items(i, groups[q])
                if q == 2:
                    value(len(waiting["V"]))
            flush_exp(99)
        while waiting["N"]:
            plan.append(waiting["N"].pop(0))
        output(i)
        return list(plan)

    return body, {kind: tail(kind) for kind in ("next", "edge", "last")}


def opening_plan():
    plan = [("WKV", ("K",), 0), ("WQ", (), 0)]
    order = [(what, ch) for what in ("K", "Q") for ch in range(BLOCKS)]
    for m, x in enumerate(order):
        plan.append(("X", x, 0))
        if m:
            plan.append(("Y", order[m - 1], 0))
        if x == ("Q", 0):
            plan.append(("WKV", ("V",), 0))
    plan.append(("Y", order[-1], 0))
    plan += [("U", (ch,), 0) for ch in range(BLOCKS)]
    plan += [("XV", (ch,), 0) for ch in range(BLOCKS)]
    plan += [("S", (q, 0), 0) for q in range(NB)]
    plan += [("E", (q, 0), 0) for q in range(NB)]
    plan += [("N", (q,), 0) for q in range(NB)]
    return plan


def bank_uses(plan):
    return [s[:2] for s in plan if s[0] in ("T", "R")]


def attention(nc, c, x, w, cos_dram, sin_dram):
    top = ExitStack()

    def sb(name, shape, dt, ctx=top):
        return ctx.enter_context(nc.sbuf_tensor(f"at_{name}", shape, dt))

    def sem(name):
        return top.enter_context(nc.semaphore(f"at_{name}"))

    body, tails = head_plan()
    uses = {kind: bank_uses(body + tail) for kind, tail in tails.items()}
    last = [("T", (BLOCKS - 1, ROWS - 1)), ("R", (BLOCKS - 1, 0)), ("R", (BLOCKS - 1, 1))]
    assert all(len(u) % SLOTS == 0 and u[-SLOTS:] == last for u in uses.values())

    with top:
        s_bank = [top.enter_context(nc.psum_tensor(f"at_s{i}", [P, BW], F32)) for i in range(BLOCKS)]
        t_bank = [top.enter_context(nc.psum_tensor(f"at_t{i}", [P, BW], F32)) for i in range(SLOTS)]
        o_bank = top.enter_context(nc.psum_tensor("at_o", [P, BW], F32))

        xt = sb("xt", [P, 2, MC, T], F32R)
        kt = sb("kt", [P, 2, T], F32R)
        qt = sb("qt", [P, 2, T], F32R)
        vv = sb("vv", [P, 2, NT, D], F32R)
        cos = sb("cos", [P, T], F32)
        sin = sb("sin", [P, T], F32)
        pt = sb("pt", [P, SLOTS, 2, BW], F32R)
        ot = sb("ot", [P, 2, BW], F32R)
        swapped = sb("swapped", [P, 2, BW], F32)
        turned = sb("turned", [P, 2, BW], F32)
        wq_raw = sb("wq_raw", [P, MC, D], F32)
        wq = sb("wq", [P, 2, MC, D], F32R)
        wkv_raw = sb("wkv_raw", [P, MC, D], F32)
        wkv = sb("wkv", [P, 2, MC, D], F32R)
        wo_raw = sb("wo_raw", [P, M], F32)
        wo = sb("wo", [P, 2, M], F32R)
        row_max = sb("row_max", [P, STATS, BLOCKS], F32)
        neg_max = sb("neg_max", [P, STATS], F32)
        row_sum = sb("row_sum", [P, STATS, BLOCKS], F32)
        inv_sum = sb("inv_sum", [P, ROWS], F32)
        early = ExitStack()
        xn = sb("xn", [P, NT, M], F32, early)
        stats = sb("stats", [P, NT, 6], F32, early)
        mv = sb("mv", [P, NT, 2], F32, early)
        small = sb("small", [P, 4, NT], F32, early)
        early.close()
        prob = [sb("prob0", [P, NB, (BLOCKS - 1) * BW], F32), sb("prob1", [P, NB, BLOCKS * BW], F32)]

        step_v, var_ready, root_done, xn_ready, xt_banked, xt_hi, xt_lo = map(
            sem, ("step_v", "var_ready", "root_done", "xn_ready", "xt_banked", "xt_hi", "xt_lo"))
        tables_loaded, wq_loaded, wkv_loaded, wo_loaded = map(sem, ("tables_loaded", "wq_loaded", "wkv_loaded", "wo_loaded"))
        wq_split, wkv_split, wo_split, split_hi = map(sem, ("wq_split", "wkv_split", "wo_split", "split_hi"))
        x_banked, x_swapped, x_cos, x_sin, x_turned, x_hi, x_lo = map(
            sem, ("x_banked", "x_swapped", "x_cos", "x_sin", "x_turned", "x_hi", "x_lo"))
        u_banked, u_copied, v_banked, v_hi, v_lo = map(sem, ("u_banked", "u_copied", "v_banked", "v_hi", "v_lo"))
        s_banked, max_part, max_ready, exp_done, sum_part, inv_ready = map(
            sem, ("s_banked", "max_part", "max_ready", "exp_done", "sum_part", "inv_ready"))
        t_banked, t_hi, t_lo, pv_done, o_hi, o_lo, r_banked = map(
            sem, ("t_banked", "t_hi", "t_lo", "pv_done", "o_hi", "o_lo", "r_banked"))
        r_added = sem("r_added")

        XG = BLOCKS * (1 + H)

        def walk(eng, steps):
            steps(opening_plan(), "next", 0, 0, 0)
            with eng.Fori(0, G - 1) as g:
                with eng.Fori(0, H - 1) as h:
                    steps(body + tails["next"], "next", g * H + h, g, h)
                steps(body + tails["edge"], "edge", g * H + H - 1, g, H - 1)
            with eng.Fori(0, H - 1) as h:
                steps(body + tails["next"], "next", (G - 1) * H + h, G - 1, h)
            steps(body + tails["last"], "last", G * H - 1, G - 1, H - 1)

        vt = prob[0][:, :, :].rearrange("p r n -> p (r n)")

        def score_bank(a, ch):
            return s_bank[chunk_no(a, ch) % BLOCKS]

        def bank_of(kind, step):
            return uses[kind].index(step) % SLOTS

        def wait_bank(eng, kind, step, hh):
            n = uses[kind].index(step) - SLOTS
            before, back = (uses[kind][n], 0) if n >= 0 else (last[n], 1)
            if before[0] == "T":
                eng.wait_ge(t_lo, (hh - back) * ITEMS + item_no(*before[1]) + 2)
            else:
                eng.wait_ge(r_added, (hh - back) * ADDS + 2 * before[1][0] + before[1][1] + 3)

        def chunk_at(kind, what, ch, g, h, nxt):
            if kind == "edge" and nxt:
                g, h = g + 1, 0
            elif nxt:
                h = h + 1
            return g * XG + ch if what == "K" else g * XG + BLOCKS + h * BLOCKS + ch

        block = top.enter_context(nc.Block())

        @block.sync
        def _(sp):
            sp.dma_start(cos[:, :], cos_dram).then_inc(tables_loaded, 16)
            sp.dma_start(sin[:, :], sin_dram).then_inc(tables_loaded, 16)

            def load_kv(which, g):
                sp.dma_start(wkv_raw[:, :, :], w[which][g].rearrange("(c p) d -> p c d", p=P)).then_inc(wkv_loaded, 16)

            def load_q(hh):
                sp.dma_start(wq_raw[:, :, :], w["q"].rearrange("g h (c p) d -> (g h) p c d", p=P)[hh]).then_inc(wq_loaded, 16)

            def load_o(hh):
                sp.dma_start(wo_raw[:, :], w["o"].rearrange("g h d m -> (g h) d m")[hh]).then_inc(wo_loaded, 16)

            load_kv("k", 0)
            load_q(0)
            load_o(0)
            sp.wait_ge(wkv_split, 1)
            load_kv("v", 0)

            def load_next(hh):
                sp.wait_ge(wq_split, hh + 1)
                load_q(hh + 1)
                sp.wait_ge(wo_split, hh + 1)
                load_o(hh + 1)

            with sp.Fori(0, G - 1) as g:
                with sp.Fori(0, H) as h:
                    load_next(g * H + h)
                sp.wait_ge(wkv_split, 2 * g + 2)
                load_kv("k", g + 1)
                sp.wait_ge(wkv_split, 2 * g + 3)
                load_kv("v", g + 1)
            with sp.Fori(0, H - 1) as h:
                load_next((G - 1) * H + h)

        @block.gpsimd
        def _(pool):
            pool.wait_ge(tables_loaded, 32)

            def steps(plan, kind, hh, g, h):
                for what, which, nxt in plan:
                    if what == "X":
                        n = chunk_at(kind, which[0], which[1], g, h, nxt)
                        r = which[1] % 2
                        cs = slice(which[1] * BW, (which[1] + 1) * BW)
                        pool.wait_ge(x_swapped, 2 * (n + 1))
                        pool.tensor_tensor(swapped[:, r, :], swapped[:, r, :], sin[:, cs], ALU.mult).then_inc(x_sin, 1)
                        pool.wait_ge(x_sin, n + 1)
                        pool.wait_ge(x_cos, n + 1)
                        pool.tensor_tensor(turned[:, r, :], turned[:, r, :], swapped[:, r, :], ALU.add).then_inc(x_turned, 1)

            walk(pool, steps)

        @block.scalar
        def _(act):
            act.wait_ge(var_ready, 1)
            nc.scalar.activation(small[:, 1, :], small[:, 0, :], ACT.Sqrt).then_inc(root_done, 1)
            for q in range(NT // 2):
                act.wait_ge(xt_banked, q + 1)
                nc.scalar.activation(xt[:, 0, :, q * 2 * P:(q + 1) * 2 * P].rearrange("p c (t j) -> p t c j", t=2),
                                     s_bank[q % BLOCKS][:, :].rearrange("p (t c j) -> p t c j", t=2, c=MC),
                                     ACT.Copy).then_inc(xt_hi, 1)

            def steps(plan, kind, hh, g, h):
                for what, which, nxt in plan:
                    if what == "X":
                        n = chunk_at(kind, which[0], which[1], g, h, nxt)
                        r = which[1] % 2
                        act.wait_ge(x_banked, n + 1)
                        act.wait_ge(x_hi, n + 1)
                        for half in range(2):
                            nc.scalar.activation(swapped[half * 64:half * 64 + 64, r, :],
                                                 s_bank[which[1]][64 - half * 64:128 - half * 64, :],
                                                 ACT.Copy).then_inc(x_swapped, 1)
                    elif what == "Y":
                        n = chunk_at(kind, which[0], which[1], g, h, nxt)
                        dst = kt if which[0] == "K" else qt
                        act.wait_ge(x_turned, n + 1)
                        nc.scalar.activation(dst[:, 0, which[1] * BW:(which[1] + 1) * BW], turned[:, which[1] % 2, :],
                                             ACT.Copy).then_inc(x_hi, 1)
                    elif what == "U":
                        ch, = which
                        act.wait_ge(u_banked, (g + nxt) * BLOCKS + ch + 1)
                        nc.scalar.activation(vt[:, ch * BW:(ch + 1) * BW], s_bank[ch][:, :], ACT.Copy).then_inc(u_copied, 1)
                    elif what == "XV":
                        ch, = which
                        gg = g + nxt
                        act.wait_ge(v_banked, gg * BLOCKS + ch + 1)
                        nc.scalar.activation(vv[:, 0, ch * NB:(ch + 1) * NB, :],
                                             s_bank[ch][:, :].rearrange("p (t d) -> p t d", t=NB), ACT.Copy).then_inc(v_hi, 1)
                    elif what == "E":
                        a, ch = which
                        width = min(BW, (a + 1) * P - ch * BW)
                        act.wait_ge(max_ready, (hh + nxt) * ROWS + a + 1)
                        nc.scalar.activation(prob[(a // NB) % 2][:, a % NB, ch * BW:ch * BW + width],
                                             score_bank(a, ch)[:, 0:width], ACT.Exp, bias=neg_max[:, a % STATS:a % STATS + 1],
                                             accum_out=row_sum[:, a % STATS, ch:ch + 1]).then_inc(exp_done, 1)
                    elif what == "T":
                        i, j = which
                        c0 = max(j - NB * i, 0) * P
                        act.wait_ge(t_banked, hh * ITEMS + item_no(i, j) + 1)
                        nc.scalar.activation(pt[:, item_no(i, j) % SLOTS, 0, c0:], t_bank[bank_of(kind, (what, which))][:, c0:],
                                             ACT.Copy).then_inc(t_hi, 1)
                    elif what == "O":
                        act.wait_ge(pv_done, hh * ITEMS + item_no(which[0], NB * (which[0] + 1) - 1) + 1)
                        nc.scalar.activation(ot[:, 0, :], o_bank[:, :], ACT.Copy).then_inc(o_hi, 1)

            walk(act, steps)

        @block.tensor
        def _(pe):
            for q in range(NT // 2):
                pe.wait_ge(xn_ready, q // 2 + 1)
                if q >= BLOCKS:
                    pe.wait_ge(xt_lo, q - BLOCKS + 1)
                for t in range(2):
                    for ch in range(MC):
                        ins = pe.transpose(s_bank[q % BLOCKS][:, (t * MC + ch) * P:(t * MC + ch + 1) * P],
                                           xn[:, 2 * q + t, ch * P:(ch + 1) * P], c["ident"][:, :])
                ins.then_inc(xt_banked, 1)
            pe.wait_ge(xt_lo, NT // 2)

            PAIRS = ((0, 0), (0, 1), (1, 0))

            def steps(plan, kind, hh, g, h):
                for what, which, nxt in plan:
                    if what == "X":
                        which_w, ch = which
                        n = chunk_at(kind, which_w, ch, g, h, nxt)
                        if ch == 0:
                            if which_w == "K":
                                pe.wait_ge(wkv_split, 2 * (g + nxt) + 1)
                            else:
                                pe.wait_ge(wq_split, hh + nxt + 1)
                        if nxt and (which_w == "K" or kind == "next"):
                            pe.wait_ge(exp_done, (hh + 1) * CHUNKS - (BLOCKS - 1 - ch))
                        if which_w == "Q":
                            if kind == "edge" or not nxt:
                                pe.wait_ge(x_cos, n - BLOCKS + 1)
                        ws = wkv if which_w == "K" else wq
                        for m, (wi, xi) in enumerate(PAIRS):
                            for mc in range(MC):
                                ins = pe.matmul(s_bank[ch][:, :], ws[:, wi, mc, :], xt[:, xi, mc, ch * BW:(ch + 1) * BW],
                                                start=m == 0 and mc == 0, stop=m == 2 and mc == MC - 1)
                        ins.then_inc(x_banked, 1)
                    elif what == "U":
                        ch, = which
                        gg = g + nxt
                        if ch == 0:
                            pe.wait_ge(wkv_split, 2 * gg + 2)
                        pe.wait_ge(x_cos, (gg * XG + BLOCKS) + ch + 1)
                        for m, (wi, xi) in enumerate(PAIRS):
                            for mc in range(MC):
                                ins = pe.matmul(s_bank[ch][:, :], wkv[:, wi, mc, :], xt[:, xi, mc, ch * BW:(ch + 1) * BW],
                                                start=m == 0 and mc == 0, stop=m == 2 and mc == MC - 1)
                        ins.then_inc(u_banked, 1)
                    elif what == "XV":
                        ch, = which
                        pe.wait_ge(u_copied, (g + nxt) * BLOCKS + ch + 1)
                        for t in range(NB):
                            ins = pe.transpose(s_bank[ch][:, t * P:(t + 1) * P], vt[:, (ch * NB + t) * P:(ch * NB + t + 1) * P],
                                               c["ident"][:, :])
                        ins.then_inc(v_banked, 1)
                    elif what == "S":
                        a, ch = which
                        i = a // NB
                        if a % NB == 0 and ch == 0:
                            n = (g * XG + BLOCKS + h * BLOCKS + i) if not nxt else chunk_at(kind, "Q", i, g, h, 1)
                            pe.wait_ge(x_lo, n + 3)
                        width = min(BW, (a + 1) * P - ch * BW)
                        n = chunk_no(a, ch)
                        if n >= BLOCKS:
                            pe.wait_ge(exp_done, (hh + nxt) * CHUNKS + n - BLOCKS + 1)
                        elif nxt and kind == "next":
                            pe.wait_ge(x_cos, chunk_at(kind, "Q", n, g, h, 1) + 1)
                        else:
                            pe.wait_ge(v_lo, (g + nxt) * BLOCKS + n + 1)
                        out = score_bank(a, ch)[:, 0:width]
                        for m, (qi, ki) in enumerate(PAIRS):
                            ins = pe.matmul(out, qt[:, qi, a * P:(a + 1) * P], kt[:, ki, ch * BW:ch * BW + width],
                                            start=m == 0, stop=m == 2 and ch < i)
                        if ch == i:
                            ins = pe.matmul(score_bank(a, ch)[:, width - P:width], c["ident16"][:, :], c["future"][:, :],
                                            start=False, stop=True)
                        ins.then_inc(s_banked, 1)
                    elif what == "T":
                        i, j = which
                        bank = t_bank[bank_of(kind, (what, which))]
                        if j % NB == 0:
                            pe.wait_ge(exp_done, hh * CHUNKS + chunk_no(NB * i + NB - 1, j // NB) + 1)
                        wait_bank(pe, kind, (what, which), hh)
                        for r in range(max(j - NB * i, 0), NB):
                            ins = pe.transpose(bank[:, r * P:(r + 1) * P],
                                               prob[i % 2][:, r, j * P:(j + 1) * P], c["ident"][:, :])
                        ins.then_inc(t_banked, 1)
                    elif what == "V":
                        i, j = which
                        slot = item_no(i, j) % SLOTS
                        c0 = max(j - NB * i, 0) * P
                        if j == 0:
                            pe.wait_ge(o_lo, hh * BLOCKS + i + 1)
                            if i == 0:
                                pe.wait_ge(v_lo, (g + 1) * BLOCKS)
                        pe.wait_ge(t_lo, hh * ITEMS + item_no(i, j) + 2)
                        for m, (vi, pi) in enumerate(PAIRS):
                            ins = pe.matmul(o_bank[:, c0:], vv[:, vi, j, :], pt[:, slot, pi, c0:],
                                            start=m == 0 and j == 0, stop=m == 2 and j == NB * (i + 1) - 1)
                        ins.then_inc(pv_done, 1)
                    elif what == "R":
                        i, half = which
                        bank = t_bank[bank_of(kind, (what, which))]
                        if half == 0:
                            pe.wait_ge(o_lo, hh * BLOCKS + i + 2)
                            if i == 0:
                                pe.wait_ge(wo_split, hh + 1)
                        wait_bank(pe, kind, (what, which), hh)
                        for t in range(2):
                            tt = half * 2 + t
                            for m, (oi, wi) in enumerate(PAIRS):
                                ins = pe.matmul(bank[:, t * M:(t + 1) * M], ot[:, oi, tt * P:(tt + 1) * P],
                                                wo[:, wi, :], start=m == 0, stop=m == 2)
                        ins.then_inc(r_banked, 1)

            walk(pe, steps)

        @block.vector
        def _(dve):
            v = Steps(dve, step_v)
            dve.engine_nop().then_inc(o_lo, 1)
            dve.engine_nop().then_inc(r_banked, 1)
            dve.engine_nop().then_inc(t_lo, 1)
            dve.engine_nop().then_inc(r_added, 2)
            dve.engine_nop().then_inc(x_hi, 2)
            dve.engine_nop().then_inc(x_lo, 2)
            layernorm(dve, v, x, None, stats, mv, small, var_ready, root_done, xn, xn_ready)
            for q in range(NT // 2):
                dve.wait_ge(xt_hi, q + 1)
                cols = slice(q * 2 * P, (q + 1) * 2 * P)
                dve.tensor_tensor(xt[:, 1, :, cols].rearrange("p c (t j) -> p t c j", t=2),
                                  s_bank[q % BLOCKS][:, :].rearrange("p (t c j) -> p t c j", t=2, c=MC),
                                  xt[:, 0, :, cols].bitcast(F32).rearrange("p c (t j) -> p t c j", t=2),
                                  ALU.subtract).then_inc(xt_lo, 1)

            def split(parts, raw, done, count):
                dve.tensor_copy(parts[:, 0], raw).then_inc(split_hi, 1)
                dve.wait_ge(split_hi, count)
                dve.tensor_tensor(parts[:, 1], raw, parts[:, 0].bitcast(F32), ALU.subtract).then_inc(done, 1)

            def steps(plan, kind, hh, g, h):
                for what, which, nxt in plan:
                    if what == "WO":
                        dve.wait_ge(wo_loaded, (hh + 1) * 16)
                        if not (isinstance(hh, int) and hh == 0):
                            dve.wait_ge(r_banked, hh * ADDS + 1)
                        split(wo, wo_raw[:, :], wo_split, 2 * hh + 2 * (g + 1) + 2)
                    elif what == "WQ":
                        if kind == "last":
                            continue
                        hn = hh + nxt
                        dve.wait_ge(wq_loaded, (hn + 1) * 16)
                        if nxt:
                            dve.wait_ge(x_banked, chunk_at("next", "Q", BLOCKS - 1, g, h, 0) + 1)
                        split(wq, wq_raw[:, :, :], wq_split, 2 * hh + 2 * (g + 1) + 3 if nxt else 2)
                    elif what == "WKV":
                        gg = g + nxt
                        k = 0 if which[0] == "K" else 1
                        dve.wait_ge(wkv_loaded, (2 * gg + k + 1) * 16)
                        if k:
                            dve.wait_ge(x_banked, gg * XG + BLOCKS)
                        elif nxt:
                            dve.wait_ge(u_banked, gg * BLOCKS)
                        n = (1 if k == 0 else 3) if not nxt else 2 * (hh + 1) + 1 + 2 * gg + k + 1
                        split(wkv, wkv_raw[:, :, :], wkv_split, n)
                    elif what == "X":
                        n = chunk_at(kind, which[0], which[1], g, h, nxt)
                        r = which[1] % 2
                        cs = slice(which[1] * BW, (which[1] + 1) * BW)
                        dve.wait_ge(x_lo, n + 1)
                        dve.wait_ge(x_swapped, 2 * (n + 1))
                        dve.tensor_tensor(turned[:, r, :], s_bank[which[1]][:, :], cos[:, cs], ALU.mult).then_inc(x_cos, 1)
                    elif what == "Y":
                        n = chunk_at(kind, which[0], which[1], g, h, nxt)
                        dst = kt if which[0] == "K" else qt
                        cs = slice(which[1] * BW, (which[1] + 1) * BW)
                        dve.wait_ge(x_hi, n + 3)
                        dve.tensor_tensor(dst[:, 1, cs], turned[:, which[1] % 2, :], dst[:, 0, cs].bitcast(F32),
                                          ALU.subtract).then_inc(x_lo, 1)
                    elif what == "XV":
                        ch, = which
                        dve.wait_ge(v_hi, (g + nxt) * BLOCKS + ch + 1)
                        dve.tensor_tensor(vv[:, 1, ch * NB:(ch + 1) * NB, :], s_bank[ch][:, :].rearrange("p (t d) -> p t d", t=NB),
                                          vv[:, 0, ch * NB:(ch + 1) * NB, :].bitcast(F32), ALU.subtract).then_inc(v_lo, 1)
                    elif what == "S":
                        a, ch = which
                        st = a % STATS
                        n = a // NB + 1
                        width = min(BW, (a + 1) * P - ch * BW)
                        dve.wait_ge(s_banked, (hh + nxt) * CHUNKS + chunk_no(a, ch) + 1)
                        out = row_max[:, st, ch:ch + 1] if n > 1 else neg_max[:, st:st + 1]
                        ins = dve.tensor_reduce(out, score_bank(a, ch)[:, 0:width], AX, ALU.max, negate=n == 1)
                        ins.then_inc(max_part if n > 1 else max_ready, 1)
                        if n > 1 and ch == n - 1:
                            dve.wait_ge(max_part, (hh + nxt) * (CHUNKS - NB) + chunk_no(a, 0) - NB + n)
                            dve.tensor_reduce(neg_max[:, st:st + 1], row_max[:, st, 0:n], AX, ALU.max, negate=True)\
                               .then_inc(max_ready, 1)
                    elif what == "N":
                        a, = which
                        st = a % STATS
                        n = a // NB + 1
                        row = (hh + nxt) * ROWS + a
                        dve.wait_ge(exp_done, (hh + nxt) * CHUNKS + chunk_no(a, n - 1) + 1)
                        if n > 1:
                            dve.tensor_reduce(row_sum[:, st, 0:1], row_sum[:, st, 0:n], AX, ALU.add).then_inc(sum_part, 1)
                            dve.wait_ge(sum_part, (hh + nxt) * (ROWS - NB) + a - NB + 1)
                        dve.reciprocal(inv_sum[:, a:a + 1], row_sum[:, st, 0:1]).then_inc(inv_ready, 1)
                    elif what == "T":
                        i, j = which
                        slot = item_no(i, j) % SLOTS
                        c0 = max(j - NB * i, 0) * P
                        dve.wait_ge(t_hi, hh * ITEMS + item_no(i, j) + 1)
                        dve.tensor_tensor(pt[:, slot, 1, c0:], t_bank[bank_of(kind, (what, which))][:, c0:],
                                          pt[:, slot, 0, c0:].bitcast(F32), ALU.subtract).then_inc(t_lo, 1)
                    elif what == "O":
                        dve.wait_ge(o_hi, hh * BLOCKS + which[0] + 1)
                        dve.tensor_tensor(ot[:, 1, :], o_bank[:, :], ot[:, 0, :].bitcast(F32), ALU.subtract).then_inc(o_lo, 1)
                    elif what == "R":
                        i, half = which
                        bank = t_bank[bank_of(kind, (what, which))]
                        tt = i * NB + half * 2
                        dve.wait_ge(r_banked, hh * ADDS + 2 * i + half + 2)
                        if half == 0:
                            dve.wait_ge(inv_ready, hh * ROWS + tt + NB)
                        for t in range(2):
                            ins = dve.scalar_tensor_tensor(x[:, tt + t, :], bank[:, t * M:(t + 1) * M], inv_sum[:, tt + t:tt + t + 1],
                                                           x[:, tt + t, :], ALU.mult, ALU.add)
                        ins.then_inc(r_added, 1)

            walk(dve, steps)


def program(nc, x_in, w_aq, w_ak, w_av, w_ao, w_cls, bias, w_gate_up, w_down, cos, sin, out):
    with ExitStack() as ctx:
        c = constants(nc, ctx)
        x = ctx.enter_context(nc.sbuf_tensor("x", [P, NT, M], F32))
        wf = {"cls": w_cls, "bias": bias, "gate_up": w_gate_up, "down": w_down}
        wa = {"q": w_aq, "k": w_ak, "v": w_av, "o": w_ao}
        ffn(nc, "ffn1", c, x, x_in[0], wf, None)
        attention(nc, c, x, wa, cos, sin)
        ffn(nc, "ffn2", c, x, None, wf, out[0])


_INS = ["L0_attn_x", "L0_attn_w_aq", "L0_attn_w_ak", "L0_attn_w_av", "L0_attn_w_ao",
        "L0_ffn_w_cls", "L0_ffn_bias", "L0_ffn_w_gate_up", "L0_ffn_w_down"]
_OUTS = [((1, T, M), "float32")]


def rotation_tables():
    half = D // 2
    freqs = np.power(np.float32(10000.0), -np.arange(half, dtype=np.float32) / np.float32(half)).astype(np.float32)
    angles = (np.arange(T, dtype=np.float32)[:, None] * freqs[None, :]).astype(np.float64)
    scale = D ** -0.25
    cos, sin = np.cos(angles).T * scale, np.sin(angles).T * scale
    return (np.ascontiguousarray(np.concatenate([cos, cos]).astype(np.float32)),
            np.ascontiguousarray(np.concatenate([-sin, sin]).astype(np.float32)))


def kernel(**inputs):
    import numpy as _np
    import concourse.bacc as _bacc
    from concourse import mybir as _mybir
    from concourse.bass_utils import run_bass_kernel_spmd as _run

    nc = _bacc.Bacc("TRN2", target_bir_lowering=False, num_devices=1)
    arrays, args = {}, []
    cos, sin = rotation_tables()
    laid = {**{name: inputs[name] for name in _INS}, "cos": cos, "sin": sin}
    for name, a in laid.items():
        a = _np.ascontiguousarray(a)
        arrays[f"in_{name}_dram"] = a
        args.append(nc.dram_tensor(f"in_{name}_dram", a.shape, _mybir.dt.from_np(a.dtype), kind="ExternalInput").ap())
    for i, (shape, dtype) in enumerate(_OUTS):
        dt = _mybir.dt.from_np(_np.dtype(dtype))
        args.append(nc.dram_tensor(f"out_{i}_dram", shape, dt, kind="ExternalOutput").ap())
    program(nc, *args)
    r = _run(nc, [arrays], core_ids=[0])
    return r.results[0]["out_0_dram"]
```
